# Optimizing a Trainium2 kernel written in Bass

```python
import numpy as np
import jax
import jax.numpy as jnp

def _softmax(x, axis=-1):
    return jax.nn.softmax(x, axis=axis)

def _gelu(x):
    return jax.nn.gelu(x, approximate=True)

def _silu(x):
    return jax.nn.silu(x)

def _sigmoid(x):
    return jax.nn.sigmoid(x)

def _layernorm(x, axis=-1, eps=1e-05):
    m = jnp.mean(x, axis=axis, keepdims=True)
    v = jnp.var(x, axis=axis, keepdims=True)
    return (x - m) / jnp.sqrt(v + eps)

def _scatter_add(tgt, idx, src, axis=0):
    return tgt.at[idx].add(src)

def _segment_sum(src, seg, n):
    return jax.ops.segment_sum(src, seg, n)
kernel_name = 'mk_cond_seq_d4_seqx_r4_eaf7a2'

def setup_inputs(seed: int=0):
    np.random.seed(seed)
    _w = jnp.asarray

    def _rec_inputs():
        import jax
        import jax.numpy as jnp
        _rk = jax.random.key(seed)
        x = -0.0005207 + 1.001 * jax.random.normal(jax.random.fold_in(_rk, 1), (16, 256, 256), jnp.float32)
        _lenS = 256 - jax.random.randint(jax.random.fold_in(_rk, 7), (16,), 0, max(1, 256 // 4) + 1, jnp.int32)
        _lenS2 = 256 - jax.random.randint(jax.random.fold_in(_rk, 8), (16,), 0, max(1, 256 // 4) + 1, jnp.int32)
        cond_2048 = 0.0061147 + 1.02565 * jax.random.normal(jax.random.fold_in(_rk, 11), (16, 512), jnp.float32)
        cond_1024 = 0.00786388 + 1.0143 * jax.random.normal(jax.random.fold_in(_rk, 12), (16, 256), jnp.float32)
        itok_S_0_1023 = jax.random.randint(jax.random.fold_in(_rk, 13), (256,), 0, 256, jnp.int32)
        _validS = jnp.arange(256)[None, :] < _lenS[:, None]
        _validS2 = jnp.arange(256)[None, :] < _lenS2[:, None]
        _causal = jnp.tril(jnp.ones((256, 256), dtype=bool))
        mask_BxS_ff1 = jnp.where(jnp.ones((16, 256), dtype=bool), 1.0, 0.0).astype(jnp.float32)
        mask_BxSx1_fk1 = jnp.where(jnp.ones((16, 256, 1), dtype=bool), 1.0, 0.0).astype(jnp.float32)
        return (x, cond_2048, cond_1024, itok_S_0_1023, mask_BxS_ff1, mask_BxSx1_fk1)
    x, cond_2048, cond_1024, itok_S_0_1023, mask_BxS_ff1, mask_BxSx1_fk1 = _rec_inputs()

    def _L0_cond_setup():
        import jax, jax.numpy as jnp
        import numpy as np
        B, S, D, E, N, R = (2, 256, 256, 512, 16, 64)
        EPS = 1e-05

        def _ln(x, g, b):
            m = jnp.mean(x, -1, keepdims=True)
            v = jnp.mean((x - m) ** 2, -1, keepdims=True)
            return (x - m) * jax.lax.rsqrt(v + EPS) * g + b

        def _ssm(u, Wdbc, Wdt, bdt, Alog, Dp):
            dbc = jnp.einsum('bse,re->bsr', u, Wdbc)
            dlt, Bm, Cm = jnp.split(dbc, [R, R + N], axis=-1)
            delta = jax.nn.softplus(jnp.einsum('bsr,er->bse', dlt, Wdt) + bdt)
            A = -jnp.exp(Alog)
            dA = jnp.exp(delta[..., None] * A)
            dBu = delta[..., None] * Bm[:, :, None, :] * u[..., None]

            def step(h, xs):
                dA_t, dBu_t, C_t = xs
                h = dA_t * h + dBu_t
                y = jnp.einsum('ben,bn->be', h, C_t)
                return (h, y)
            h0 = jnp.zeros((u.shape[0], u.shape[2], N), u.dtype)
            _, ys = jax.lax.scan(step, h0, (dA.swapaxes(0, 1), dBu.swapaxes(0, 1), Cm.swapaxes(0, 1)))
            return ys.swapaxes(0, 1) + u * Dp
        key = jax.random.key(seed)
        ks = jax.random.split(key, 16)
        f = lambda k, sh, s=0.02: jax.random.normal(k, sh, jnp.float32) * s
        Alog = jnp.log(jnp.tile(jnp.arange(1, N + 1, dtype=jnp.float32), (E, 1)))
        return dict(x=f(ks[0], (B, S, D), 1.0), c=f(ks[1], (B, 2 * D), 1.0), w=f(ks[2], (B, D), 1.0), norm1_g=jnp.ones((D,)), norm1_b=jnp.zeros((D,)), norm2_g=jnp.ones((D,)), norm2_b=jnp.zeros((D,)), Wx=f(ks[3], (E, D)), bx=jnp.zeros((E,)), Wz=f(ks[4], (E, D)), bz=jnp.zeros((E,)), Wf=f(ks[5], (D, E)), bf=jnp.zeros((D,)), Wada=f(ks[6], (3 * D, 2 * D)), bada=jnp.zeros((3 * D,)), Wc1=f(ks[7], (E, E)), bc1=jnp.zeros((E,)), Wc2=f(ks[8], (E, E)), bc2=jnp.zeros((E,)), Wdbc1=f(ks[9], (R + 2 * N, E)), Wdt1=f(ks[10], (E, R)), bdt1=jnp.zeros((E,)), Alog1=Alog, Dp1=jnp.ones((E,)), Wdbc2=f(ks[11], (R + 2 * N, E)), Wdt2=f(ks[12], (E, R)), bdt2=jnp.zeros((E,)), Alog2=Alog, Dp2=jnp.ones((E,)))
    _L0_cond_all = _L0_cond_setup()
    _L0_cond_in = {k: v for k, v in _L0_cond_all.items() if k in ('norm1_g', 'norm1_b', 'norm2_g', 'norm2_b', 'Wx', 'bx', 'Wz', 'bz', 'Wf', 'bf', 'Wada', 'bada', 'Wc1', 'bc1', 'Wc2', 'bc2', 'Wdbc1', 'Wdt1', 'bdt1', 'Alog1', 'Dp1', 'Wdbc2', 'Wdt2', 'bdt2', 'Alog2', 'Dp2')}
    del _L0_cond_all

    def _L1_cond_setup():
        import jax, jax.numpy as jnp
        import numpy as np
        B_SZ, S, D = (4, 256, 256)
        DI, DS, DTR, DC = (512, 16, 64, 4)
        EPS = 1e-05

        def _layernorm(x, g, b):
            m = jnp.mean(x, axis=-1, keepdims=True)
            v = jnp.var(x, axis=-1, keepdims=True)
            return (x - m) * jax.lax.rsqrt(v + EPS) * g + b

        def _mamba(h, W_in, conv_w, conv_b, W_xp, W_dt, b_dt, A_log, D_param, W_out):
            bsz = h.shape[0]
            xz = h @ W_in
            xm, z = jnp.split(xz, 2, axis=-1)
            xc = jnp.transpose(xm, (0, 2, 1))
            xc = jax.lax.conv_general_dilated(xc, conv_w, (1,), [(DC - 1, 0)], feature_group_count=DI, dimension_numbers=('NCH', 'OIH', 'NCH'))
            xc = xc + conv_b[None, :, None]
            xm = jax.nn.silu(jnp.transpose(xc, (0, 2, 1)))
            xdbl = xm @ W_xp
            dtr, Bm, Cm = jnp.split(xdbl, [DTR, DTR + DS], axis=-1)
            dt = jax.nn.softplus(dtr @ W_dt + b_dt)
            A = -jnp.exp(A_log)

            def step(hst, inp):
                dt_t, B_t, C_t, x_t = inp
                dA = jnp.exp(dt_t[:, :, None] * A)
                hst = hst * dA + (dt_t * x_t)[:, :, None] * B_t[:, None, :]
                y = jnp.einsum('bds,bs->bd', hst, C_t)
                return (hst, y)
            inputs = (jnp.transpose(dt, (1, 0, 2)), jnp.transpose(Bm, (1, 0, 2)), jnp.transpose(Cm, (1, 0, 2)), jnp.transpose(xm, (1, 0, 2)))
            h0 = jnp.zeros((bsz, DI, DS), dt.dtype)
            _, ys = jax.lax.scan(step, h0, inputs)
            y = jnp.transpose(ys, (1, 0, 2)) + xm * D_param
            y = y * jax.nn.silu(z)
            return y @ W_out
        key = jax.random.key(seed)
        ks = jax.random.split(key, 12)

        def w(k, shape, scale=0.02):
            return jax.random.normal(k, shape, jnp.float32) * scale
        x = jax.random.normal(ks[0], (B_SZ, S, D), jnp.float32)
        c = jax.random.normal(ks[1], (B_SZ, 2 * D), jnp.float32)
        W_ada = w(ks[2], (2 * D, 3 * D))
        b_ada = jnp.zeros((3 * D,), jnp.float32)
        gamma = jnp.ones((D,), jnp.float32)
        beta = jnp.zeros((D,), jnp.float32)
        W_in = w(ks[3], (D, 2 * DI))
        conv_w = w(ks[4], (DI, 1, DC), 0.1)
        conv_b = jnp.zeros((DI,), jnp.float32)
        W_xp = w(ks[5], (DI, DTR + 2 * DS))
        W_dt = w(ks[6], (DTR, DI))
        b_dt = jnp.full((DI,), jnp.log(jnp.expm1(jnp.float32(0.01))), jnp.float32)
        A_log = jnp.log(jnp.broadcast_to(jnp.arange(1, DS + 1, dtype=jnp.float32), (DI, DS)))
        D_param = jnp.ones((DI,), jnp.float32)
        W_out = w(ks[7], (DI, D))
        perm = jax.random.permutation(ks[8], S)
        inv_perm = jnp.argsort(perm)
        return dict(x=x, c=c, W_ada=W_ada, b_ada=b_ada, gamma=gamma, beta=beta, W_in=W_in, conv_w=conv_w, conv_b=conv_b, W_xp=W_xp, W_dt=W_dt, b_dt=b_dt, A_log=A_log, D_param=D_param, W_out=W_out, perm=perm, inv_perm=inv_perm)
    _L1_cond_all = _L1_cond_setup()
    _L1_cond_in = {k: v for k, v in _L1_cond_all.items() if k in ('W_ada', 'b_ada', 'gamma', 'beta', 'W_in', 'conv_w', 'conv_b', 'W_xp', 'W_dt', 'b_dt', 'A_log', 'D_param', 'W_out')}
    del _L1_cond_all

    def _L2_cond_setup():
        import jax, jax.numpy as jnp
        import numpy as np
        B, T, D, H, TE = (8, 256, 256, 16, 512)
        LN_EPS = 1e-05

        def layer_norm(x, w, b):
            m = jnp.mean(x, axis=-1, keepdims=True)
            v = jnp.var(x, axis=-1, keepdims=True)
            return (x - m) / jnp.sqrt(v + LN_EPS) * w + b
        key = jax.random.key(seed)
        ks = jax.random.split(key, 8)
        s = lambda k, sh: jax.random.normal(k, sh, jnp.float32) * 0.02
        return dict(x=jax.random.normal(ks[0], (B, T, D), jnp.float32), emb=jax.random.normal(ks[1], (B, TE), jnp.float32), src_mask=jnp.ones((B, T), jnp.float32), norm_w=jnp.ones((D,), jnp.float32), norm_b=jnp.zeros((D,), jnp.float32), q_w=s(ks[2], (D, D)), q_b=jnp.zeros((D,), jnp.float32), k_w=s(ks[3], (D, D)), k_b=jnp.zeros((D,), jnp.float32), v_w=s(ks[4], (D, D)), v_b=jnp.zeros((D,), jnp.float32), emb_w=s(ks[5], (TE, 2 * D)), emb_b=jnp.zeros((2 * D,), jnp.float32), sb_norm_w=jnp.ones((D,), jnp.float32), sb_norm_b=jnp.zeros((D,), jnp.float32), out_w=s(ks[6], (D, D)), out_b=jnp.zeros((D,), jnp.float32))
    _L2_cond_all = _L2_cond_setup()
    _L2_cond_in = {k: v for k, v in _L2_cond_all.items() if k in ('norm_w', 'norm_b', 'q_w', 'q_b', 'k_w', 'k_b', 'v_w', 'v_b', 'emb_w', 'emb_b', 'sb_norm_w', 'sb_norm_b', 'out_w', 'out_b')}
    del _L2_cond_all

    def _L3_cond_setup():
        import jax, jax.numpy as jnp
        import numpy as np
        B, T, D, H, TE = (4, 512, 256, 8, 512)
        EPS = 1e-05

        def _ln(x, w, b):
            m = jnp.mean(x, axis=-1, keepdims=True)
            v = jnp.mean((x - m) ** 2, axis=-1, keepdims=True)
            return (x - m) * jax.lax.rsqrt(v + EPS) * w + b
        key = jax.random.key(seed)
        ks = jax.random.split(key, 16)
        s = 0.02
        inp = {'x': jax.random.normal(ks[0], (B, T, D), jnp.float32), 'emb': jax.random.normal(ks[1], (B, TE), jnp.float32), 'src_mask': (jax.random.uniform(ks[2], (B, T, 1)) > 0.2).astype(jnp.float32), 'num_head': H, 'ln_w': jnp.ones((D,), jnp.float32), 'ln_b': jnp.zeros((D,), jnp.float32), 'Wq': jax.random.normal(ks[3], (D, D), jnp.float32) * s, 'bq': jnp.zeros((D,), jnp.float32), 'Wk': jax.random.normal(ks[4], (D, D), jnp.float32) * s, 'bk': jnp.zeros((D,), jnp.float32), 'Wv': jax.random.normal(ks[5], (D, D), jnp.float32) * s, 'bv': jnp.zeros((D,), jnp.float32), 'W_emb': jax.random.normal(ks[6], (TE, 2 * D), jnp.float32) * s, 'b_emb': jnp.zeros((2 * D,), jnp.float32), 'ln2_w': jnp.ones((D,), jnp.float32), 'ln2_b': jnp.zeros((D,), jnp.float32), 'W_out': jax.random.normal(ks[7], (D, D), jnp.float32) * s, 'b_out': jnp.zeros((D,), jnp.float32)}
        return inp
    _L3_cond_all = _L3_cond_setup()
    _L3_cond_in = {k: v for k, v in _L3_cond_all.items() if k in ('ln_w', 'ln_b', 'Wq', 'bq', 'Wk', 'bk', 'Wv', 'bv', 'W_emb', 'b_emb', 'ln2_w', 'ln2_b', 'W_out', 'b_out')}
    del _L3_cond_all
    return {'x': x, 'cond_2048': cond_2048, 'cond_1024': cond_1024, 'itok_S_0_1023': itok_S_0_1023, 'mask_BxS_ff1': mask_BxS_ff1, 'mask_BxSx1_fk1': mask_BxSx1_fk1, 'L0_cond_norm1_g': _L0_cond_in['norm1_g'], 'L0_cond_norm1_b': _L0_cond_in['norm1_b'], 'L0_cond_norm2_g': _L0_cond_in['norm2_g'], 'L0_cond_norm2_b': _L0_cond_in['norm2_b'], 'L0_cond_Wx': _L0_cond_in['Wx'], 'L0_cond_bx': _L0_cond_in['bx'], 'L0_cond_Wz': _L0_cond_in['Wz'], 'L0_cond_bz': _L0_cond_in['bz'], 'L0_cond_Wf': _L0_cond_in['Wf'], 'L0_cond_bf': _L0_cond_in['bf'], 'L0_cond_Wada': _L0_cond_in['Wada'], 'L0_cond_bada': _L0_cond_in['bada'], 'L0_cond_Wc1': _L0_cond_in['Wc1'], 'L0_cond_bc1': _L0_cond_in['bc1'], 'L0_cond_Wc2': _L0_cond_in['Wc2'], 'L0_cond_bc2': _L0_cond_in['bc2'], 'L0_cond_Wdbc1': _L0_cond_in['Wdbc1'], 'L0_cond_Wdt1': _L0_cond_in['Wdt1'], 'L0_cond_bdt1': _L0_cond_in['bdt1'], 'L0_cond_Alog1': _L0_cond_in['Alog1'], 'L0_cond_Dp1': _L0_cond_in['Dp1'], 'L0_cond_Wdbc2': _L0_cond_in['Wdbc2'], 'L0_cond_Wdt2': _L0_cond_in['Wdt2'], 'L0_cond_bdt2': _L0_cond_in['bdt2'], 'L0_cond_Alog2': _L0_cond_in['Alog2'], 'L0_cond_Dp2': _L0_cond_in['Dp2'], 'L1_cond_W_ada': _L1_cond_in['W_ada'], 'L1_cond_b_ada': _L1_cond_in['b_ada'], 'L1_cond_gamma': _L1_cond_in['gamma'], 'L1_cond_beta': _L1_cond_in['beta'], 'L1_cond_W_in': _L1_cond_in['W_in'], 'L1_cond_conv_w': _L1_cond_in['conv_w'], 'L1_cond_conv_b': _L1_cond_in['conv_b'], 'L1_cond_W_xp': _L1_cond_in['W_xp'], 'L1_cond_W_dt': _L1_cond_in['W_dt'], 'L1_cond_b_dt': _L1_cond_in['b_dt'], 'L1_cond_A_log': _L1_cond_in['A_log'], 'L1_cond_D_param': _L1_cond_in['D_param'], 'L1_cond_W_out': _L1_cond_in['W_out'], 'L2_cond_norm_w': _L2_cond_in['norm_w'], 'L2_cond_norm_b': _L2_cond_in['norm_b'], 'L2_cond_q_w': _L2_cond_in['q_w'], 'L2_cond_q_b': _L2_cond_in['q_b'], 'L2_cond_k_w': _L2_cond_in['k_w'], 'L2_cond_k_b': _L2_cond_in['k_b'], 'L2_cond_v_w': _L2_cond_in['v_w'], 'L2_cond_v_b': _L2_cond_in['v_b'], 'L2_cond_emb_w': _L2_cond_in['emb_w'], 'L2_cond_emb_b': _L2_cond_in['emb_b'], 'L2_cond_sb_norm_w': _L2_cond_in['sb_norm_w'], 'L2_cond_sb_norm_b': _L2_cond_in['sb_norm_b'], 'L2_cond_out_w': _L2_cond_in['out_w'], 'L2_cond_out_b': _L2_cond_in['out_b'], 'L3_cond_ln_w': _L3_cond_in['ln_w'], 'L3_cond_ln_b': _L3_cond_in['ln_b'], 'L3_cond_Wq': _L3_cond_in['Wq'], 'L3_cond_bq': _L3_cond_in['bq'], 'L3_cond_Wk': _L3_cond_in['Wk'], 'L3_cond_bk': _L3_cond_in['bk'], 'L3_cond_Wv': _L3_cond_in['Wv'], 'L3_cond_bv': _L3_cond_in['bv'], 'L3_cond_W_emb': _L3_cond_in['W_emb'], 'L3_cond_b_emb': _L3_cond_in['b_emb'], 'L3_cond_ln2_w': _L3_cond_in['ln2_w'], 'L3_cond_ln2_b': _L3_cond_in['ln2_b'], 'L3_cond_W_out': _L3_cond_in['W_out'], 'L3_cond_b_out': _L3_cond_in['b_out']}

def reference(x, cond_2048, cond_1024, itok_S_0_1023, mask_BxS_ff1, mask_BxSx1_fk1, L0_cond_norm1_g, L0_cond_norm1_b, L0_cond_norm2_g, L0_cond_norm2_b, L0_cond_Wx, L0_cond_bx, L0_cond_Wz, L0_cond_bz, L0_cond_Wf, L0_cond_bf, L0_cond_Wada, L0_cond_bada, L0_cond_Wc1, L0_cond_bc1, L0_cond_Wc2, L0_cond_bc2, L0_cond_Wdbc1, L0_cond_Wdt1, L0_cond_bdt1, L0_cond_Alog1, L0_cond_Dp1, L0_cond_Wdbc2, L0_cond_Wdt2, L0_cond_bdt2, L0_cond_Alog2, L0_cond_Dp2, L1_cond_W_ada, L1_cond_b_ada, L1_cond_gamma, L1_cond_beta, L1_cond_W_in, L1_cond_conv_w, L1_cond_conv_b, L1_cond_W_xp, L1_cond_W_dt, L1_cond_b_dt, L1_cond_A_log, L1_cond_D_param, L1_cond_W_out, L2_cond_norm_w, L2_cond_norm_b, L2_cond_q_w, L2_cond_q_b, L2_cond_k_w, L2_cond_k_b, L2_cond_v_w, L2_cond_v_b, L2_cond_emb_w, L2_cond_emb_b, L2_cond_sb_norm_w, L2_cond_sb_norm_b, L2_cond_out_w, L2_cond_out_b, L3_cond_ln_w, L3_cond_ln_b, L3_cond_Wq, L3_cond_bq, L3_cond_Wk, L3_cond_bk, L3_cond_Wv, L3_cond_bv, L3_cond_W_emb, L3_cond_b_emb, L3_cond_ln2_w, L3_cond_ln2_b, L3_cond_W_out, L3_cond_b_out):
    import jax
    import jax.numpy as jnp

    def _L0_cond_ref(x, c, w, norm1_g, norm1_b, norm2_g, norm2_b, Wx, bx, Wz, bz, Wf, bf, Wada, bada, Wc1, bc1, Wc2, bc2, Wdbc1, Wdt1, bdt1, Alog1, Dp1, Wdbc2, Wdt2, bdt2, Alog2, Dp2):
        import jax, jax.numpy as jnp
        import numpy as np
        B, S, D, E, N, R = (2, 256, 256, 512, 16, 64)
        EPS = 1e-05

        def _ln(x, g, b):
            m = jnp.mean(x, -1, keepdims=True)
            v = jnp.mean((x - m) ** 2, -1, keepdims=True)
            return (x - m) * jax.lax.rsqrt(v + EPS) * g + b

        def _ssm(u, Wdbc, Wdt, bdt, Alog, Dp):
            dbc = jnp.einsum('bse,re->bsr', u, Wdbc)
            dlt, Bm, Cm = jnp.split(dbc, [R, R + N], axis=-1)
            delta = jax.nn.softplus(jnp.einsum('bsr,er->bse', dlt, Wdt) + bdt)
            A = -jnp.exp(Alog)
            dA = jnp.exp(delta[..., None] * A)
            dBu = delta[..., None] * Bm[:, :, None, :] * u[..., None]

            def step(h, xs):
                dA_t, dBu_t, C_t = xs
                h = dA_t * h + dBu_t
                y = jnp.einsum('ben,bn->be', h, C_t)
                return (h, y)
            h0 = jnp.zeros((u.shape[0], u.shape[2], N), u.dtype)
            _, ys = jax.lax.scan(step, h0, (dA.swapaxes(0, 1), dBu.swapaxes(0, 1), Cm.swapaxes(0, 1)))
            return ys.swapaxes(0, 1) + u * Dp
        ada = jax.nn.silu(c) @ Wada.T + bada
        shift, scale, gate = jnp.split(ada, 3, axis=1)
        x_ssm = _ln(x, norm1_g, norm1_b)
        x_ssm = x_ssm * (1.0 + scale[:, None, :]) + shift[:, None, :]
        skip = x_ssm
        x_ssm = _ln(x_ssm, norm2_g, norm2_b)
        mz = jnp.einsum('bsd,ed->bse', x_ssm, Wz) + bz
        mx = jnp.einsum('bsd,ed->bse', x_ssm, Wx) + bx
        act_mx = jax.nn.silu(mx)
        z1 = jnp.einsum('bse,fe->bsf', mz, Wc1) + bc1
        z1 = _ssm(z1, Wdbc1, Wdt1, bdt1, Alog1, Dp1)
        y1 = act_mx * z1
        z2 = jnp.einsum('bse,fe->bsf', mz, Wc2) + bc2
        z2 = jnp.flip(z2, axis=1)
        z2 = _ssm(z2, Wdbc2, Wdt2, bdt2, Alog2, Dp2)
        z2 = jnp.flip(z2, axis=1)
        y2 = act_mx * z2
        out = jnp.einsum('bse,de->bsd', y1 + y2, Wf) + bf + skip
        return x + gate[:, None, :] * out

    def _L1_cond_ref(x, c, W_ada, b_ada, gamma, beta, W_in, conv_w, conv_b, W_xp, W_dt, b_dt, A_log, D_param, W_out, perm, inv_perm):
        import jax, jax.numpy as jnp
        import numpy as np
        B_SZ, S, D = (4, 256, 256)
        DI, DS, DTR, DC = (512, 16, 64, 4)
        EPS = 1e-05

        def _layernorm(x, g, b):
            m = jnp.mean(x, axis=-1, keepdims=True)
            v = jnp.var(x, axis=-1, keepdims=True)
            return (x - m) * jax.lax.rsqrt(v + EPS) * g + b

        def _mamba(h, W_in, conv_w, conv_b, W_xp, W_dt, b_dt, A_log, D_param, W_out):
            bsz = h.shape[0]
            xz = h @ W_in
            xm, z = jnp.split(xz, 2, axis=-1)
            xc = jnp.transpose(xm, (0, 2, 1))
            xc = jax.lax.conv_general_dilated(xc, conv_w, (1,), [(DC - 1, 0)], feature_group_count=DI, dimension_numbers=('NCH', 'OIH', 'NCH'))
            xc = xc + conv_b[None, :, None]
            xm = jax.nn.silu(jnp.transpose(xc, (0, 2, 1)))
            xdbl = xm @ W_xp
            dtr, Bm, Cm = jnp.split(xdbl, [DTR, DTR + DS], axis=-1)
            dt = jax.nn.softplus(dtr @ W_dt + b_dt)
            A = -jnp.exp(A_log)

            def step(hst, inp):
                dt_t, B_t, C_t, x_t = inp
                dA = jnp.exp(dt_t[:, :, None] * A)
                hst = hst * dA + (dt_t * x_t)[:, :, None] * B_t[:, None, :]
                y = jnp.einsum('bds,bs->bd', hst, C_t)
                return (hst, y)
            inputs = (jnp.transpose(dt, (1, 0, 2)), jnp.transpose(Bm, (1, 0, 2)), jnp.transpose(Cm, (1, 0, 2)), jnp.transpose(xm, (1, 0, 2)))
            h0 = jnp.zeros((bsz, DI, DS), dt.dtype)
            _, ys = jax.lax.scan(step, h0, inputs)
            y = jnp.transpose(ys, (1, 0, 2)) + xm * D_param
            y = y * jax.nn.silu(z)
            return y @ W_out
        mod = jax.nn.silu(c) @ W_ada + b_ada
        shift, scale, gate = jnp.split(mod, 3, axis=1)
        h = _layernorm(x, gamma, beta)
        h = h * (1.0 + scale[:, None, :]) + shift[:, None, :]
        h = h[:, perm]
        y = _mamba(h, W_in, conv_w, conv_b, W_xp, W_dt, b_dt, A_log, D_param, W_out)
        y = y[:, inv_perm]
        return x + gate[:, None, :] * y

    def _L2_cond_ref(x, emb, src_mask, norm_w, norm_b, q_w, q_b, k_w, k_b, v_w, v_b, emb_w, emb_b, sb_norm_w, sb_norm_b, out_w, out_b):
        import jax, jax.numpy as jnp
        import numpy as np
        B, T, D, H, TE = (8, 256, 256, 16, 512)
        LN_EPS = 1e-05

        def layer_norm(x, w, b):
            m = jnp.mean(x, axis=-1, keepdims=True)
            v = jnp.var(x, axis=-1, keepdims=True)
            return (x - m) / jnp.sqrt(v + LN_EPS) * w + b
        Bx, Tx, Dx = x.shape
        xn = layer_norm(x, norm_w, norm_b)
        q = (xn @ q_w + q_b).reshape(Bx, Tx, H, -1)
        k = (xn @ k_w + k_b).reshape(Bx, Tx, H, -1)
        att = jnp.einsum('bnhl,bmhl->bnmh', q, k)
        mask = src_mask.reshape(Bx, 1, Tx, 1)
        att = att + (1.0 - mask) * -1000000.0
        att = jax.nn.softmax(att, axis=2)
        v = ((xn @ v_w + v_b) * src_mask[:, :, None]).reshape(Bx, Tx, H, -1)
        y = jnp.einsum('bnmh,bmhl->bnhl', att, v).reshape(Bx, Tx, Dx)
        e = jax.nn.silu(emb) @ emb_w + emb_b
        scale, shift = jnp.split(e[:, None, :], 2, axis=2)
        h = layer_norm(y, sb_norm_w, sb_norm_b) * (1.0 + scale) + shift
        h = jax.nn.silu(h) @ out_w + out_b
        return x + h

    def _L3_cond_ref(x, emb, src_mask, num_head, ln_w, ln_b, Wq, bq, Wk, bk, Wv, bv, W_emb, b_emb, ln2_w, ln2_b, W_out, b_out):
        import jax, jax.numpy as jnp
        import numpy as np
        B, T, D, H, TE = (4, 512, 256, 8, 512)
        EPS = 1e-05

        def _ln(x, w, b):
            m = jnp.mean(x, axis=-1, keepdims=True)
            v = jnp.mean((x - m) ** 2, axis=-1, keepdims=True)
            return (x - m) * jax.lax.rsqrt(v + EPS) * w + b
        b, t, d = x.shape
        h = num_head
        dh = d // h
        xn = _ln(x, ln_w, ln_b)
        q = xn @ Wq + bq
        k = xn @ Wk + bk + (1.0 - src_mask) * -1000000.0
        q = jax.nn.softmax(q.reshape(b, t, h, dh), axis=-1)
        k = jax.nn.softmax(k.reshape(b, t, h, dh), axis=1)
        v = ((xn @ Wv + bv) * src_mask).reshape(b, t, h, dh)
        att = jnp.einsum('bnhd,bnhl->bhdl', k, v)
        y = jnp.einsum('bnhd,bhdl->bnhl', q, att).reshape(b, t, d)
        emb_out = (jax.nn.silu(emb) @ W_emb + b_emb)[:, None, :]
        scale, shift = jnp.split(emb_out, 2, axis=2)
        hh = _ln(y, ln2_w, ln2_b) * (1.0 + scale) + shift
        hh = jax.nn.silu(hh) @ W_out + b_out
        return x + hh
    x = _L0_cond_ref(x, cond_2048, cond_1024, L0_cond_norm1_g, L0_cond_norm1_b, L0_cond_norm2_g, L0_cond_norm2_b, L0_cond_Wx, L0_cond_bx, L0_cond_Wz, L0_cond_bz, L0_cond_Wf, L0_cond_bf, L0_cond_Wada, L0_cond_bada, L0_cond_Wc1, L0_cond_bc1, L0_cond_Wc2, L0_cond_bc2, L0_cond_Wdbc1, L0_cond_Wdt1, L0_cond_bdt1, L0_cond_Alog1, L0_cond_Dp1, L0_cond_Wdbc2, L0_cond_Wdt2, L0_cond_bdt2, L0_cond_Alog2, L0_cond_Dp2)
    x = _L1_cond_ref(x, cond_2048, L1_cond_W_ada, L1_cond_b_ada, L1_cond_gamma, L1_cond_beta, L1_cond_W_in, L1_cond_conv_w, L1_cond_conv_b, L1_cond_W_xp, L1_cond_W_dt, L1_cond_b_dt, L1_cond_A_log, L1_cond_D_param, L1_cond_W_out, itok_S_0_1023, itok_S_0_1023)
    x = _L2_cond_ref(x, cond_2048, mask_BxS_ff1, L2_cond_norm_w, L2_cond_norm_b, L2_cond_q_w, L2_cond_q_b, L2_cond_k_w, L2_cond_k_b, L2_cond_v_w, L2_cond_v_b, L2_cond_emb_w, L2_cond_emb_b, L2_cond_sb_norm_w, L2_cond_sb_norm_b, L2_cond_out_w, L2_cond_out_b)
    x = _L3_cond_ref(x, cond_2048, mask_BxSx1_fk1, 8, L3_cond_ln_w, L3_cond_ln_b, L3_cond_Wq, L3_cond_bq, L3_cond_Wk, L3_cond_bk, L3_cond_Wv, L3_cond_bv, L3_cond_W_emb, L3_cond_b_emb, L3_cond_ln2_w, L3_cond_ln2_b, L3_cond_W_out, L3_cond_b_out)
    return x

_drawn_inputs = setup_inputs


def setup_inputs(seed=0):
    import zlib

    import numpy as np

    out = dict(_drawn_inputs(seed))
    spreads = {'L0_cond_norm1_g': (1.0, 0.2),
     'L0_cond_norm1_b': (0.0, 0.1),
     'L0_cond_norm2_g': (1.0, 0.2),
     'L0_cond_norm2_b': (0.0, 0.1),
     'L0_cond_bx': (0.0, 0.1),
     'L0_cond_bz': (0.0, 0.1),
     'L0_cond_bf': (0.0, 0.1),
     'L0_cond_bada': (0.0, 0.1),
     'L0_cond_bc1': (0.0, 0.1),
     'L0_cond_bc2': (0.0, 0.1),
     'L0_cond_bdt1': (0.0, 0.1),
     'L0_cond_Dp1': (1.0, 0.2),
     'L0_cond_bdt2': (0.0, 0.1),
     'L0_cond_Dp2': (1.0, 0.2),
     'L1_cond_b_ada': (0.0, 0.1),
     'L1_cond_gamma': (1.0, 0.2),
     'L1_cond_beta': (0.0, 0.1),
     'L1_cond_conv_b': (0.0, 0.1),
     'L1_cond_b_dt': (-4.600166320800781, 0.2),
     'L1_cond_D_param': (1.0, 0.2),
     'L2_cond_norm_w': (1.0, 0.2),
     'L2_cond_norm_b': (0.0, 0.1),
     'L2_cond_q_b': (0.0, 0.1),
     'L2_cond_k_b': (0.0, 0.1),
     'L2_cond_v_b': (0.0, 0.1),
     'L2_cond_emb_b': (0.0, 0.1),
     'L2_cond_sb_norm_w': (1.0, 0.2),
     'L2_cond_sb_norm_b': (0.0, 0.1),
     'L2_cond_out_b': (0.0, 0.1),
     'L3_cond_ln_w': (1.0, 0.2),
     'L3_cond_ln_b': (0.0, 0.1),
     'L3_cond_bq': (0.0, 0.1),
     'L3_cond_bk': (0.0, 0.1),
     'L3_cond_bv': (0.0, 0.1),
     'L3_cond_b_emb': (0.0, 0.1),
     'L3_cond_ln2_w': (1.0, 0.2),
     'L3_cond_ln2_b': (0.0, 0.1),
     'L3_cond_b_out': (0.0, 0.1)}
    factors = {}
    for name, (base, spread) in spreads.items():
        noise = np.random.default_rng([zlib.crc32(name.encode()), seed]).standard_normal(out[name].shape)
        drawn = base * np.exp(spread * noise) if base else spread * noise
        out[name] = jnp.asarray(drawn.astype(out[name].dtype))
    for name, factor in factors.items():
        out[name] = (out[name] * factor).astype(out[name].dtype)
    return out
```

```python
from contextlib import ExitStack

import numpy as np

import concourse.bass as bass
from concourse import mybir

F32 = mybir.dt.float32
I32 = mybir.dt.int32
ALU = mybir.AluOpType
ACT = mybir.ActivationFunctionType
AX = mybir.AxisListType

P = 128
B, T, D = 16, 256, 256
E, N, R = 512, 16, 64
TB, DB, EB = T // P, D // P, E // P
CT = 4
C2 = 2 * D
CB_ = C2 // P
H2, DH2 = 16, D // 16
HPB = 4
H3, DH3 = 8, D // 8
EPS = 1e-5
NEG = 1e6
HALF = EB // 2
UNITS = (EB // HALF) * N
LAG = 4
RESET = 1e37
ADAW = [3 * D, 3 * D, 2 * D, 2 * D]
NADA = sum(ADAW)

WEIGHTS = dict(wx=(DB, E), wf=(EB, D), wdlt0=(EB, R), wbc0=(EB, 2 * N), wdlt1=(EB, R), wbc1=(EB, 2 * N),
               win=(DB, 2 * E), wdlt2=(EB, R), wbc2=(EB, 2 * N), wout1=(EB, D),
               wq2=(DB, 4 * P), wk2=(DB, 4 * P), wv2=(DB, D), wo2=(DB, D),
               wq3=(DB, D), wk3=(DB, D), wv3=(DB, D), wo3=(DB, D))
COLUMNS = dict(n2g=DB, n2b=DB, bx=EB, bz=EB, bc0=EB, bc1=EB, bdt0=EB, bdt1=EB, bdt2=EB,
               dp0=EB, dp1=EB, dp2=EB, alog0=EB * N, alog1=EB * N, alog2=EB * N,
               convw=EB * CT, convb=EB, l2w=DB, l2b=DB, bq2=4, bk2=4, l3w=DB, l3b=DB, bk3=DB,
               mask2=B * TB, mask3=B * TB, keyrow=1)
BIASROWS = ["bf", "bv2", "bo2", "bq3", "bv3", "bo3"]
NORMROWS = 8


def offsets(widths):
    at, out = 0, {}
    for name, w in widths.items():
        out[name] = (at, w)
        at += w
    return out, at


WOFF, WTOT = offsets({k: a * b for k, (a, b) in WEIGHTS.items()})
COFF, CTOT = offsets(COLUMNS)

SEMS = """
loaded consts cond_act ada_full ada_taken ada_bias rows_ready rows_stored cols_full cols_taken alog_exp alog_done
fold_full fold_taken foldb_full foldb_done gather_ready itok_f
dve_chain act_chain pool_chain
b_full dbu_done c_full c_taken da_ready scan_done g_ready g_used skip_done y_full y_taken key_in q_sb k_sb
x_in row_in gate_in out_done cols_now
xn_a xt_full_a xt_sb_a mx_full mx_sb z_full z_sb
dlt_full dlt_sb dt_read bc_full bc_sb dt_full sp_clip sp_log delta_done
yb_full_0 yg_0 o_full_0 res_0
xn_b xt_full_b xt_sb_b xm_full xm_sb gz_full gz_sb conv_acc conv_done conv_silu
yb_full_1 yg_1 o_full_1 o_sb_1 og_full_1 res_1
xn_c xt_full_c xt_sb_c qk_full v2_full v2_sb s_full s_max p_ready pt_full pt_sb o_full_2 o_taken_2
yn_2 yt_full_2 yt_sb_2 h_full_2 res_2
xn_d xt_full_d xt_sb_d qkv_full v3_sb q_sub q_exp k_sub k_exp qk3_t qk3_sb bd_full bd_sb y3_full yn_3 yt_full_3 yt_sb_3
h_full_3 res_3 mask_in
""".split()


def build(nc, dram, out):
    with ExitStack() as ctx:
        def sb(name, shape, dt=F32):
            return ctx.enter_context(nc.sbuf_tensor(name, shape, dt))

        def ps(name, shape):
            return ctx.enter_context(nc.psum_tensor(name, shape, F32))

        S = {n: ctx.enter_context(nc.semaphore(n)) for n in SEMS}
        sem_nums = [v.num for v in S.values()]
        assert sem_nums == list(range(sem_nums[0], sem_nums[0] + len(SEMS)))
        all_sems = range(sem_nums[0], sem_nums[-1] + 1)

        mod_rows = nc.dram_tensor("mod_rows", (B, 4 * D), F32, kind="Internal").ap()

        W = sb("weights", [P, WTOT])
        w = {k: W[:, WOFF[k][0]:WOFF[k][0] + a * b].rearrange("p (k m) -> p k m", k=a)
             for k, (a, b) in WEIGHTS.items()}
        CO = sb("columns", [P, CTOT])
        c = {k: CO[:, o:o + n] for k, (o, n) in COFF.items()}
        wdt = sb("wdt", [R, 3, E])
        brow = sb("bias_rows", [1, len(BIASROWS), D])
        z1w = sb("z1w", [P, DB, E])
        z2w = sb("z2w", [P, DB, E])
        z1b = sb("z1b", [P, EB])
        z2b = sb("z2b", [P, EB])
        acoef = sb("acoef", [P, 3, EB, N])
        mod_cols = sb("mod_cols", [P, 6 * DB, B])
        ident = sb("ident", [P, P])
        ones = sb("ones", [1, P])
        gath = sb("gather", [P, TB, T])
        blockmask = sb("blockmask", [P, P])

        ps_da = ps("ps_da", [P, 2, HALF, T])
        ps_b = ps("ps_b", [P, 512])
        ps_c = ps("ps_c", [P, 512])
        ps_y = ps("ps_y", [P, TB, HALF * P])
        ps_w = ps("ps_w", [P, 3, 512])

        def bank(k, m=None):
            return ps_w[:, k, :] if m is None else ps_w[:, k, :].rearrange("p (a n) -> p a n", a=m)

        with ExitStack() as pro:
            def sbp(name, shape, dt=F32):
                return pro.enter_context(nc.sbuf_tensor(name, shape, dt))

            ada_w = sbp("ada_w", [P, CB_, NADA])
            ada_b = sbp("ada_b", [1, NADA])
            cond = sbp("cond", [P, CB_, B])
            cond_s = sbp("cond_s", [P, CB_, B])
            norm_rows = sbp("norm_rows", [B, NORMROWS, D])
            mods = sbp("mods", [B, NADA])
            rows = sbp("rows", [B, 10, D])
            scaled = sbp("scaled", [B, 4, D])
            wz = sbp("wz", [P, EB, D])
            wc = sbp("wc", [P, 2, EB, E])
            itok_i = sbp("itok_i", [P, T], I32)
            itok = sbp("itok", [P, T])
            token = sbp("token", [P, TB])

            with nc.Block() as block:
                loads = [(W[:, :], dram["weights"]), (CO[:, :], dram["columns"]),
                         (wdt[:, :, :], dram["wdt"]), (brow[:, :, :], dram["bias_rows"]),
                         (ada_w[:, :, :], dram["ada_w"]), (ada_b[:, :], dram["ada_b"]),
                         (cond[:, :, :], dram["cond"]),
                         (norm_rows[:, :, :], dram["norm_rows"].partition_broadcast(B)),
                         (wz[:, :, :], dram["wz"]), (wc[:, :, :, :], dram["wc"]),
                         (itok_i[:, :], dram["itok"].partition_broadcast(P))]
                ALL_LOADED = 16 * len(loads)

                @block.sync
                def _(sp):
                    for dst, src in loads:
                        sp.dma_start(dst, src).then_inc(S["loaded"], 16)
                    sp.wait_ge(S["rows_ready"], 1)
                    sp.dma_start(mod_rows, rows[:, 0:4, :].rearrange("b r d -> b (r d)")).then_inc(S["rows_stored"], 16)
                    sp.wait_ge(S["rows_stored"], 16)

                @block.gpsimd
                def _(pool):
                    n = 0

                    def done(ins):
                        nonlocal n
                        n += 1
                        ins.then_inc(S["pool_chain"], 1)
                        pool.wait_ge(S["pool_chain"], n)

                    done(pool.memset(ident[:, :], 0.0))
                    done(pool.affine_select(out=ident[:, :], in_=ident[:, :], compare_op=ALU.not_equal, fill=1.0,
                                            base=0, pattern=[[-1, P]], channel_multiplier=1))
                    done(pool.memset(ones[:, :], 1.0))
                    done(pool.memset(blockmask[:, :], 1.0))
                    by_head = blockmask[:, :].rearrange("p (h l) -> p h l", l=DH3)
                    done(pool.affine_select(out=by_head, in_=by_head, compare_op=ALU.is_ge, fill=0.0, base=0,
                                            pattern=[[-DH3, P // DH3], [0, DH3]], channel_multiplier=1))
                    done(pool.affine_select(out=by_head, in_=by_head, compare_op=ALU.is_ge, fill=0.0, base=DH3 - 1,
                                            pattern=[[DH3, P // DH3], [0, DH3]], channel_multiplier=-1))
                    done(pool.iota(token[:, :], pattern=[[P, TB]], base=0, channel_multiplier=1,
                                   allow_small_or_imprecise_dtypes=True))
                    pool.nop().then_inc(S["consts"], 1)

                @block.scalar
                def _(act):
                    act.wait_ge(S["loaded"], ALL_LOADED)
                    nc.scalar.activation(cond_s[:, :, :], cond[:, :, :], ACT.Silu).then_inc(S["cond_act"], 1)
                    for j in range(NADA // 512):
                        act.wait_ge(S["ada_full"], j + 1)
                        nc.scalar.activation(mods[:, j * 512:(j + 1) * 512], ps_w[0:B, j % 2, :],
                                             ACT.Copy).then_inc(S["ada_taken"], 1)
                    for j, dst in enumerate((z1w, z1w, z2w, z2w)):
                        act.wait_ge(S["fold_full"], j + 1)
                        nc.scalar.activation(dst[:, j % 2, :], ps_w[:, j % 2, :], ACT.Copy).then_inc(S["fold_taken"], 1)
                    for s, a in enumerate((c["alog0"], c["alog1"], c["alog2"])):
                        nc.scalar.activation(acoef[:, s, :, :], a.rearrange("p (e n) -> p e n", n=N),
                                             ACT.Exp).then_inc(S["alog_exp"], 1)

                @block.tensor
                def _(pe):
                    pe.wait_ge(S["loaded"], ALL_LOADED)
                    pe.wait_ge(S["consts"], 1)
                    pe.wait_ge(S["cond_act"], 1)
                    for j in range(NADA // 512):
                        if j >= 2:
                            pe.wait_ge(S["ada_taken"], j - 1)
                        for k in range(CB_):
                            nc.tensor.matmul(ps_w[0:B, j % 2, :], cond_s[:, k, :], ada_w[:, k, j * 512:(j + 1) * 512],
                                             start=(k == 0), stop=False)
                        nc.tensor.matmul(ps_w[0:B, j % 2, :], ones[0:1, 0:B], ada_b[:, j * 512:(j + 1) * 512],
                                         start=False, stop=True).then_inc(S["ada_full"], 1)
                    for j in range(2 * DB):
                        if j == 0:
                            pe.wait_ge(S["ada_taken"], NADA // 512)
                        if j >= 2:
                            pe.wait_ge(S["fold_taken"], j - 1)
                        for k in range(EB):
                            last = nc.tensor.matmul(ps_w[:, j % 2, :], wz[:, k, (j % DB) * P:(j % DB + 1) * P],
                                                    wc[:, j // DB, k, :], start=(k == 0), stop=(k == EB - 1))
                        last.then_inc(S["fold_full"], 1)
                    for s in range(2):
                        for m in range(EB):
                            for k in range(EB):
                                last = nc.tensor.matmul(ps_c[:, s * EB + m:s * EB + m + 1],
                                                        wc[:, s, k, m * P:(m + 1) * P], c["bz"][:, k:k + 1],
                                                        start=(k == 0), stop=(k == EB - 1))
                    last.then_inc(S["foldb_full"], 1)
                    pe.wait_ge(S["rows_ready"], 1)
                    for r in range(6):
                        for d in range(DB):
                            q = r * DB + d
                            last = nc.tensor.matmul(ps_b[:, q * B:(q + 1) * B], rows[:, 4 + r, d * P:(d + 1) * P],
                                                    ident[0:B, 0:B], is_transpose=True, start=True, stop=True)
                    last.then_inc(S["cols_full"], 1)

                @block.vector
                def _(dve):
                    n = 0

                    def done(ins):
                        nonlocal n
                        n += 1
                        ins.then_inc(S["dve_chain"], 1)
                        dve.wait_ge(S["dve_chain"], n)

                    dve.wait_ge(S["loaded"], ALL_LOADED)
                    dve.wait_ge(S["consts"], 1)
                    done(nc.vector.tensor_copy(itok[:, :], itok_i[:, :]))
                    for k in range(TB):
                        nc.vector.tensor_scalar(gath[:, k, :], itok[:, :], token[:, k:k + 1], None,
                                                ALU.is_equal).then_inc(S["gather_ready"], 1)
                    dve.wait_ge(S["ada_taken"], NADA // 512)
                    at = 0
                    where = []
                    for width in ADAW:
                        where.append(at)
                        at += width
                    for layer, (lo, dst) in enumerate(zip(where, (0, 4, 6, 8))):
                        sc = lo + (D if layer < 2 else 0)
                        sh = lo + (0 if layer < 2 else D)
                        gain, shift = norm_rows[:, 2 * layer, :], norm_rows[:, 2 * layer + 1, :]
                        nc.vector.scalar_tensor_tensor(out=rows[:, dst, :], in0=mods[:, sc:sc + D], scalar=1.0,
                                                       in1=gain, op0=ALU.add, op1=ALU.mult)
                        done(nc.vector.scalar_tensor_tensor(out=scaled[:, layer, :], in0=mods[:, sc:sc + D], scalar=1.0,
                                                            in1=shift, op0=ALU.add, op1=ALU.mult))
                        done(nc.vector.tensor_tensor(rows[:, dst + 1, :], scaled[:, layer, :], mods[:, sh:sh + D],
                                                     ALU.add))
                    for layer in range(2):
                        done(nc.vector.tensor_copy(rows[:, 2 + layer, :],
                                                   mods[:, where[layer] + 2 * D:where[layer] + 3 * D]))
                    nc.vector.engine_nop().then_inc(S["rows_ready"], 1)
                    dve.wait_ge(S["foldb_full"], 1)
                    nc.vector.tensor_tensor(z1b[:, :], ps_c[:, 0:EB], c["bc0"], ALU.add)
                    nc.vector.tensor_tensor(z2b[:, :], ps_c[:, EB:2 * EB], c["bc1"], ALU.add).then_inc(S["foldb_done"], 1)
                    dve.wait_ge(S["cols_full"], 1)
                    nc.vector.tensor_copy(mod_cols[:, :, :].rearrange("p q b -> p (q b)"),
                                          ps_b[:, 0:6 * DB * B]).then_inc(S["cols_taken"], 1)
                    dve.wait_ge(S["alog_exp"], 3)
                    a = acoef[:, :, :, :].rearrange("p s e n -> p (s e n)")
                    nc.vector.tensor_scalar(a, a, -1.0, None, ALU.mult).then_inc(S["alog_done"], 1)
                    dve.wait_ge(S["gather_ready"], TB)
                    dve.wait_ge(S["foldb_done"], 1)
                    dve.wait_ge(S["cols_taken"], 1)
                    dve.wait_ge(S["alog_done"], 1)
                    dve.wait_ge(S["fold_taken"], 4)
            nc.multi_engine_barrier(list(mybir.ALL_ENGINES), sems_to_clear=all_sems)

        u_s = [sb(f"u{s}", [P, EB, T]) for s in range(3)]
        delta = [sb(f"delta{s}", [P, EB, T]) for s in range(3)]
        du = [sb(f"du{s}", [P, EB, T]) for s in range(3)]
        bcm = [sb(f"bcm{s}", [P, TB, 2 * N]) for s in range(3)]
        dlt = sb("dlt", [R, T])
        soft = sb("soft", [P, EB, T])
        soft2 = sb("soft2", [P, EB, T])
        c_bc = sb("c_bc", [P, N, T])
        dbu = sb("dbu", [P, 2, HALF, T])
        hst = sb("hst", [P, 3, HALF, T])
        g = sb("g", [P, 2, HALF, T])
        yt = [sb(f"yt{s}", [P, TB, E]) for s in range(3)]
        x0 = sb("x0", [P, TB, D])
        x1 = sb("x1", [P, TB, D])
        xr = sb("xr", [P, TB, D])
        x2 = sb("x2", [P, TB, D])
        xa = sb("xa", [P, TB, D])
        xn = sb("xn", [P, TB, D])
        xT = sb("xT", [P, DB, T])
        rows_bc = sb("rows_bc", [P, 3, D])
        gate1 = sb("gate1", [P, D])
        act_x = sb("act_x", [P, EB, T])
        act_z = sb("act_z", [P, EB, T])
        yg = sb("yg", [P, EB, T])
        xm = sb("xm", [P, EB, CT - 1 + T])
        acc = sb("acc", [P, EB, T])
        tmp = sb("tmp", [P, TB, D])
        cols1 = sb("cols1", [P, 2 * DB])
        cols23 = sb("cols23", [P, 4 * DB])
        masks = sb("masks", [P, 2 * TB])
        st = sb("stats", [P, 4, TB, 6])
        mv = sb("mv", [P, 4, TB, 2])
        nrm = sb("nrm", [P, 4, 6, TB])
        qT, kT = soft, soft2
        v2 = sb("v2", [P, TB, H2, DH2 + 1])
        sc_s = xm[:, :, :].rearrange("p e t -> p (e t)")[:, 0:4 * T].rearrange("p (a q t) -> p a q t", a=2, q=TB)
        mx = sb("mx", [P, 2, 2, TB])
        pr = acc[:, :, :].rearrange("p (a q) t -> p a q t", a=2)
        pT = yg[:, :, :].rearrange("p (a q) t -> p a q t", a=2)
        rec = sb("rec", [P, 2, TB, H2 // 2])
        yv = sb("yv", [P, TB, D])
        maskrow = sb("maskrow", [P, T])
        keymask = maskrow
        r3 = sb("r3", [P, 4, 16])
        bd = sb("bd", [P, DB, P])
        kmax = sb("kmax", [P, 4, DB])

        class Chain:

            def __init__(self, eng, sem):
                self.eng, self.sem, self.n = eng, sem, 0

            def mark(self, ins):
                self.n += 1
                ins.then_inc(self.sem, 1)
                return self.n

            def done(self, ins):
                self.eng.wait_ge(self.sem, self.mark(ins))

        class Scan:
            def __init__(self, s, backward=False):
                self.s, self.backward = s, backward

            def order(self, ap):
                flat = ap.rearrange("p e t -> p (e t)")
                return flat[:, HALF * T - 1::-1] if self.backward else flat

            def tensor(self, pe, tick):
                s = self.s
                for u in range(UNITS + LAG):
                    if u < UNITS:
                        n = u % N
                        if u >= 1:
                            pe.wait_ge(S["dbu_done"], u)
                        for t in range(TB):
                            last = nc.tensor.matmul(ps_b[:, t * P:(t + 1) * P],
                                                    bcm[s][:, t, n:n + 1].broadcast_to([P, P]), ident[:, :],
                                                    is_transpose=True, start=True, stop=True)
                        last.then_inc(S["b_full"], 1)
                        if u < N:
                            if n >= 1:
                                pe.wait_ge(S["c_taken"], n)
                            for t in range(TB):
                                last = nc.tensor.matmul(ps_c[:, t * P:(t + 1) * P],
                                                        bcm[s][:, t, N + n:N + n + 1].broadcast_to([P, P]),
                                                        ident[:, :], is_transpose=True, start=True, stop=True)
                            last.then_inc(S["c_full"], 1)
                    if u >= LAG:
                        self.sum_states(pe, u - LAG)
                    tick()

            def sum_states(self, pe, u):
                hh, n = u // N, u % N
                if n == 0:
                    if hh >= 1:
                        pe.wait_ge(S["y_taken"], hh)
                    for t in range(TB):
                        for e in range(HALF):
                            last = nc.tensor.matmul(ps_y[:, t, e * P:(e + 1) * P],
                                                    u_s[self.s][:, hh * HALF + e, t * P:(t + 1) * P], ident[:, :],
                                                    is_transpose=True, start=(t == 0 and e == 0), stop=False,
                                                    skip_group_check=True)
                pe.wait_ge(S["g_ready"], u + 1)
                for t in range(TB):
                    for e in range(HALF):
                        last = nc.tensor.matmul(ps_y[:, t, e * P:(e + 1) * P],
                                                g[:, u % 2, e, t * P:(t + 1) * P], ident[:, :],
                                                is_transpose=True, start=False, stop=(n == N - 1),
                                                skip_group_check=True)
                last.then_inc(S["g_used"], 1)

            def scalar(self, act, tick):
                s = self.s
                for u in range(UNITS):
                    hh, n = u // N, u % N
                    if u >= 2:
                        act.wait_ge(S["scan_done"], u - 1)
                    for e in range(HALF):
                        eb = hh * HALF + e
                        last = nc.scalar.activation(ps_da[:, u % 2, e, :], delta[s][:, eb, :], ACT.Exp,
                                                    scale=acoef[:, s, eb, n:n + 1])
                    last.then_inc(S["da_ready"], 1)
                    if u < N:
                        act.wait_ge(S["c_full"], n + 1)
                        nc.scalar.activation(c_bc[:, n, :], ps_c[:, 0:T], ACT.Copy).then_inc(S["c_taken"], 1)
                    if u == N + LAG - 1:
                        self.take(act, 0)
                    tick()
                self.take(act, 1)

            def take(self, act, hh):
                act.wait_ge(S["g_used"], (hh + 1) * N)
                nc.scalar.activation(yt[self.s][:, :, hh * HALF * P:(hh + 1) * HALF * P], ps_y[:, :, :],
                                     ACT.Copy).then_inc(S["y_taken"], 1)

            def vector(self, dve, tick):
                s = self.s
                for u in range(UNITS + 1):
                    if u < UNITS:
                        hh = u // N
                        dve.wait_ge(S["b_full"], u + 1)
                        if u >= 2:
                            dve.wait_ge(S["scan_done"], u - 1)
                        nc.vector.tensor_tensor(dbu[:, u % 2, :, :], du[s][:, hh * HALF:(hh + 1) * HALF, :],
                                                ps_b[:, 0:T].unsqueeze(1).broadcast_to([P, HALF, T]),
                                                ALU.mult).then_inc(S["dbu_done"], 1)
                    if u >= 1:
                        v = u - 1
                        dve.wait_ge(S["dbu_done"], u)
                        dve.wait_ge(S["da_ready"], u)
                        if v >= 3:
                            dve.wait_ge(S["g_ready"], v - 2)
                        nc.vector.tensor_tensor_scan(self.order(hst[:, v % 3, :, :]), self.order(ps_da[:, v % 2, :, :]),
                                                     self.order(dbu[:, v % 2, :, :]), 0.0, ALU.mult,
                                                     ALU.add).then_inc(S["scan_done"], 1)
                    tick()

            def gpsimd(self, pool):
                for u in range(UNITS):
                    n = u % N
                    pool.wait_ge(S["scan_done"], u + 1)
                    if u < N:
                        pool.wait_ge(S["c_taken"], n + 1)
                    if u >= 2:
                        pool.wait_ge(S["g_used"], u - 1)
                    nc.gpsimd.tensor_tensor(g[:, u % 2, :, :], hst[:, u % 3, :, :],
                                            c_bc[:, n, :].unsqueeze(1).broadcast_to([P, HALF, T]),
                                            ALU.mult).then_inc(S["g_ready"], 1)
                pool.wait_ge(S["y_taken"], EB // HALF)
                pool.wait_ge(S["g_used"], UNITS)

        def norm(ch, slot, src, scale_shift):
            ve = nc.vector
            for t in range(TB):
                last = ch.mark(ve.bn_stats(st[:, slot, t, :], src[:, t, :]))
            ch.eng.wait_ge(ch.sem, last)
            for t in range(TB):
                last = ch.mark(ve.bn_aggr(mv[:, slot, t, :], st[:, slot, t, :]))
            ch.eng.wait_ge(ch.sem, last)
            k = nrm[:, slot, :, :]
            ch.done(ve.tensor_scalar(k[:, 0, :], mv[:, slot, :, 1], EPS, None, ALU.add))
            ch.mark(ve.tensor_scalar(k[:, 1, :], k[:, 0, :], -0.5, None, ALU.mult))
            ch.done(ve.tensor_scalar(k[:, 2, :].bitcast(I32), k[:, 0, :].bitcast(I32), -0.5, 1597463007.0,
                                     ALU.mult, ALU.add))
            a, b = 2, 3
            for _ in range(3):
                ch.done(ve.tensor_tensor(k[:, 4, :], k[:, a, :], k[:, a, :], ALU.mult))
                ch.done(ve.tensor_tensor(k[:, 5, :], k[:, 4, :], k[:, 1, :], ALU.mult))
                ch.done(ve.scalar_tensor_tensor(out=k[:, b, :], in0=k[:, 5, :], scalar=1.5, in1=k[:, a, :],
                                                op0=ALU.add, op1=ALU.mult))
                a, b = b, a
            for t in range(TB):
                last = scale_shift(t, mv[:, slot, t, 0:1], k[:, a, t:t + 1])
            return last

        def plain(src):
            def go(t, mean, inv):
                return nc.vector.tensor_scalar(xn[:, t, :], src[:, t, :], mean, inv, ALU.subtract, ALU.mult)
            return go

        def turn(src, k, full):
            for d in range(DB):
                for t in range(TB):
                    last = nc.tensor.matmul(bank(k, DB)[:, d, t * P:(t + 1) * P], src[:, t, d * P:(d + 1) * P],
                                            ident[:, :], is_transpose=True, start=True, stop=True)
            last.then_inc(full, 1)

        def project(dst, weight, m0, m, rhs, kb):
            for k in range(kb):
                last = nc.tensor.matmul(dst, weight[:, k, m0:m0 + m], rhs[:, k, :], start=(k == 0), stop=(k == kb - 1))
            return last

        def to_tokens(dst, lhs, t, weight, kb, bias=None):
            for k in range(kb):
                last = nc.tensor.matmul(dst, lhs[:, k, t * P:(t + 1) * P], weight[:, k, :], start=(k == 0),
                                        stop=(bias is None and k == kb - 1))
            if bias is not None:
                last = nc.tensor.matmul(dst, ones[0:1, :], brow[0:1, BIASROWS.index(bias), :], start=False, stop=True)
            return last

        def prep_tensor(pe, s, r, ready, count, t0):
            pe.wait_ge(ready, count)
            if r >= 1:
                pe.wait_ge(S["bc_sb"], r)
            project(ps_w[0:R, 1, P:P + T], (w["wdlt0"], w["wdlt1"], w["wdlt2"])[s], 0, R, u_s[s], EB).then_inc(S["dlt_full"], 1)
            pe.wait_ge(S["dlt_full"], r + 1)
            yield t0 + 1
            for t in range(TB):
                last = to_tokens(bank(1)[:, t * 2 * N:(t + 1) * 2 * N], u_s[s], t, (w["wbc0"], w["wbc1"], w["wbc2"])[s], EB)
            last.then_inc(S["bc_full"], 1)
            yield t0 + 3
            pe.wait_ge(S["dlt_sb"], r + 1)
            if r >= 1:
                pe.wait_ge(S["dt_read"], r)
            for k, pair in ((2, (0, 1)), (0, (2, 3))):
                for j, eb in enumerate(pair):
                    last = nc.tensor.matmul(bank(k, 2)[:, j, :], wdt[:, s, eb * P:(eb + 1) * P], dlt[:, :],
                                            start=True, stop=True)
                last.then_inc(S["dt_full"], 1)
            yield t0 + 4

        def prep_scalar(act, s, r, t0):
            act.wait_ge(S["bc_full"], r + 1)
            if r >= 1:
                act.wait_ge(S["dt_full"], 2 * r)
            nc.scalar.activation(dlt[:, :], ps_w[0:R, 1, P:P + T], ACT.Copy).then_inc(S["dlt_sb"], 1)
            nc.scalar.activation(bcm[s][:, :, :].rearrange("p t n -> p (t n)"), bank(1)[:, 0:TB * 2 * N],
                                 ACT.Copy).then_inc(S["bc_sb"], 1)
            yield t0 + 5
            act.wait_ge(S["sp_clip"], r + 1)
            ch = act_chain[0]
            ch.done(nc.scalar.activation(soft2[:, :, :], soft[:, :, :], ACT.Exp))
            nc.scalar.activation(soft[:, :, :], soft2[:, :, :], ACT.Ln, bias=1.0).then_inc(S["sp_log"], 1)
            yield t0 + 6

        def prep_vector(dve, ch, s, r, edge, t0):
            bdt = (c["bdt0"], c["bdt1"], c["bdt2"])[s]
            for k, pair in ((2, (0, 1)), (0, (2, 3))):
                dve.wait_ge(S["dt_full"], 2 * r + (1 if k == 2 else 2))
                for j, eb in enumerate(pair):
                    last = nc.vector.tensor_scalar(soft[:, eb, :], bank(k, 2)[:, j, :], bdt[:, eb:eb + 1], 30.0,
                                                   ALU.add, ALU.min)
                    ch.mark(last) if eb < EB - 1 else last.then_inc(S["sp_clip"], 1)
            yield t0 + 6
            dve.wait_ge(S["sp_log"], r + 1)
            for k, pair in ((2, (0, 1)), (0, (2, 3))):
                for j, eb in enumerate(pair):
                    last = ch.mark(nc.vector.scalar_tensor_tensor(
                        out=delta[s][:, eb, :], in0=bank(k, 2)[:, j, :], scalar=bdt[:, eb:eb + 1],
                        in1=soft[:, eb, :], op0=ALU.add, op1=ALU.max))
            dve.wait_ge(S["dve_chain"], last)
            nc.vector.engine_nop().then_inc(S["dt_read"], 1)
            yield t0 + 7
            ch.done(nc.vector.tensor_tensor(du[s][:, :, :], delta[s][:, :, :], u_s[s][:, :, :], ALU.mult))
            yield t0 + 8
            for eb in range(EB):
                nc.vector.tensor_scalar(u_s[s][:, eb, :], u_s[s][:, eb, :], (c["dp0"], c["dp1"], c["dp2"])[s][:, eb:eb + 1],
                                        None, ALU.mult).then_inc(S["skip_done"], 1)
            nc.vector.memset(delta[s][:, :, edge:edge + 1], RESET).then_inc(S["delta_done"], 1)
            dve.wait_ge(S["skip_done"], (r + 1) * EB)
            yield t0 + 8

        def l0_pre_sync(sp, b):
            sp.dma_start(x0[:, :, :], dram["x"][bass.ds(b, 1)].rearrange("b (k p) d -> p (b k) d", p=P)).then_inc(S["x_in"], 16)
            sp.dma_start(rows_bc[:, :, :].rearrange("p r d -> p (r d)"),
                         mod_rows[bass.ds(b, 1), 0:3 * D].rearrange("b d -> (b d)").partition_broadcast(P)).then_inc(S["row_in"], 16)

        def l0_pre_vector(dve, ch, t0):
            dve.wait_ge(S["x_in"], 16)
            dve.wait_ge(S["row_in"], 16)

            def modulate(t, mean, inv):
                ch.done(nc.vector.scalar_tensor_tensor(out=tmp[:, t, :], in0=x0[:, t, :], scalar=mean,
                                                       in1=rows_bc[:, 0, :], op0=ALU.subtract, op1=ALU.mult))
                return nc.vector.scalar_tensor_tensor(out=xa[:, t, :], in0=tmp[:, t, :], scalar=inv,
                                                      in1=rows_bc[:, 1, :], op0=ALU.mult, op1=ALU.add)

            ch.done(norm(ch, 0, x0, modulate))
            yield t0 + 2
            norm(ch, 1, xa, plain(xa)).then_inc(S["xn_a"], 1)
            yield t0 + 16
            yield from prep_vector(dve, ch, 0, 0, 0, t0 + 12)
            yield t0 + 20
            yield from prep_vector(dve, ch, 1, 1, T - 1, t0 + 16)

        def l0_pre_tensor(pe, t0):
            pe.wait_ge(S["xn_a"], 1)
            turn(xn, 0, S["xt_full_a"])
            yield t0 + 5
            pe.wait_ge(S["xt_sb_a"], 1)
            for k in range(2):
                for j in range(2):
                    last = project(bank(1 + k, 2)[:, j, :], w["wx"], (2 * k + j) * P, P, xT, DB)
                last.then_inc(S["mx_full"], 1)
                yield t0 + 6 + k
            for k in range(4):
                if k == 1:
                    pe.wait_ge(S["mx_sb"], 2)
                if k == 3:
                    pe.wait_ge(S["z_sb"], 1)
                for j in range(2):
                    last = project(bank((0, 1, 2, 0)[k], 2)[:, j, :], (z1w, z2w)[k // 2], (2 * (k % 2) + j) * P, P, xT, DB)
                last.then_inc(S["z_full"], 1)
                yield t0 + 8 + k
            yield t0 + 12
            pe.wait_ge(S["z_sb"], 4)
            yield from prep_tensor(pe, 0, 0, S["z_sb"], 4, t0 + 12)
            yield from prep_tensor(pe, 1, 1, S["z_sb"], 4, t0 + 16)

        def l0_pre_scalar(act, t0):
            act.wait_ge(S["xt_full_a"], 1)
            for d in range(DB):
                last = nc.scalar.activation(xT[:, d, :], bank(0, DB)[:, d, :], ACT.Identity, scale=c["n2g"][:, d:d + 1],
                                            bias=c["n2b"][:, d:d + 1])
            last.then_inc(S["xt_sb_a"], 1)
            yield t0 + 7
            for k in range(2):
                act.wait_ge(S["mx_full"], k + 1)
                for j in range(2):
                    eb = 2 * k + j
                    last = nc.scalar.activation(act_x[:, eb, :], bank(1 + k, 2)[:, j, :], ACT.Silu, bias=c["bx"][:, eb:eb + 1])
                last.then_inc(S["mx_sb"], 1)
                yield t0 + 7 + k
            for k in range(4):
                act.wait_ge(S["z_full"], k + 1)
                for j in range(2):
                    eb = 2 * (k % 2) + j
                    last = nc.scalar.activation(u_s[k // 2][:, eb, :], bank((0, 1, 2, 0)[k], 2)[:, j, :], ACT.Identity,
                                                bias=(z1b, z2b)[k // 2][:, eb:eb + 1])
                last.then_inc(S["z_sb"], 1)
                yield t0 + 9 + k
            yield t0 + 14
            yield from prep_scalar(act, 0, 0, t0 + 12)
            yield t0 + 18
            yield from prep_scalar(act, 1, 1, t0 + 16)

        def l0_post_tensor(pe, t0):
            for k in range(2):
                for j in range(2):
                    eb = 2 * k + j
                    for t in range(TB):
                        for s in range(2):
                            last = nc.tensor.matmul(bank(k, 2)[:, j, t * P:(t + 1) * P],
                                                    yt[s][:, t, eb * P:(eb + 1) * P], ident[:, :], is_transpose=True,
                                                    start=(j == 0 and t == 0 and s == 0), stop=(s == 1),
                                                    skip_group_check=True)
                last.then_inc(S["yb_full_0"], 1)
            yield t0 + 2
            pe.wait_ge(S["yg_0"], 2)
            for t in range(TB):
                last = to_tokens(bank(2, TB)[:, t, :], yg, t, w["wf"], EB, "bf")
                if t == 0:
                    yield t0 + 3
            last.then_inc(S["o_full_0"], 1)
            yield t0 + 5
            pe.wait_ge(S["res_0"], 1)
            yield t0 + 5

        def l0_post_vector(dve, ch, t0):
            for k in range(2):
                dve.wait_ge(S["yb_full_0"], k + 1)
                nc.vector.tensor_tensor(yg[:, 2 * k:2 * k + 2, :], bank(k, 2), act_x[:, 2 * k:2 * k + 2, :],
                                        ALU.mult).then_inc(S["yg_0"], 1)
            yield t0 + 4
            dve.wait_ge(S["o_full_0"], 1)
            ch.done(nc.vector.tensor_tensor(tmp[:, :, :], bank(2, TB), xa[:, :, :], ALU.add))
            ch.done(nc.vector.tensor_tensor(x1[:, :, :], tmp[:, :, :],
                                            rows_bc[:, 2, :].unsqueeze(1).broadcast_to([P, TB, D]), ALU.mult))
            ins = nc.vector.tensor_tensor(x1[:, :, :], x1[:, :, :], x0[:, :, :], ALU.add)
            ins.then_inc(S["res_0"], 1)
            dve.wait_ge(S["res_0"], 1)
            yield t0 + 5

        def l1_pre_vector(dve, ch, b, t0):
            ch.done(nc.vector.tensor_copy(xr[:, :, :], x1[:, :, :]))
            nc.vector.tensor_copy(cols1[:, :].unsqueeze(2), mod_cols[:, 0:2 * DB, bass.ds(b, 1)]).then_inc(S["cols_now"], 1)
            norm(ch, 2, x1, plain(x1)).then_inc(S["xn_b"], 1)
            yield t0 + 4
            nc.vector.memset(xm[:, :, 0:CT - 1], 0.0)
            for k in range(2):
                dve.wait_ge(S["xm_full"], k + 1)
                ch.mark(nc.vector.tensor_copy(xm[:, 2 * k:2 * k + 2, CT - 1:CT - 1 + T], bank(1 + k, 2)))
                for j in range(2):
                    eb = 2 * k + j
                    last = nc.vector.tensor_scalar(acc[:, eb, :], bank(1 + k, 2)[:, j, :],
                                                   c["convw"][:, eb * CT + CT - 1:eb * CT + CT], c["convb"][:, eb:eb + 1],
                                                   ALU.mult, ALU.add)
                last.then_inc(S["xm_sb"], 1)
                yield t0 + 5 + k
            dve.wait_ge(S["xm_sb"], 2)
            yield t0 + 6
            for tap in range(CT - 1):
                for eb in range(EB):
                    last = nc.vector.scalar_tensor_tensor(
                        out=acc[:, eb, :], in0=xm[:, eb, tap:tap + T], scalar=c["convw"][:, eb * CT + tap:eb * CT + tap + 1],
                        in1=acc[:, eb, :], op0=ALU.mult, op1=ALU.add)
                    last.then_inc(S["conv_done"], 1)
                dve.wait_ge(S["conv_done"], (tap + 1) * EB)
                yield t0 + 7 + tap
            yield t0 + 14
            yield from prep_vector(dve, ch, 2, 0, 0, t0 + 10)

        def l1_pre_tensor(pe, t0):
            pe.wait_ge(S["xn_b"], 1)
            for d in range(DB):
                for t in range(TB):
                    last = nc.tensor.matmul(bank(0, DB)[:, d, :], xn[:, t, d * P:(d + 1) * P], gath[:, t, :],
                                            start=(t == 0), stop=(t == TB - 1))
            last.then_inc(S["xt_full_b"], 1)
            yield t0 + 3
            pe.wait_ge(S["xt_sb_b"], 1)
            for k in range(2):
                for j in range(2):
                    last = project(bank(1 + k, 2)[:, j, :], w["win"], (2 * k + j) * P, P, xT, DB)
                last.then_inc(S["xm_full"], 1)
                yield t0 + 4 + k
            for k in range(2):
                if k == 1:
                    pe.wait_ge(S["xm_sb"], 1)
                for j in range(2):
                    last = project(bank(k, 2)[:, j, :], w["win"], E + (2 * k + j) * P, P, xT, DB)
                last.then_inc(S["gz_full"], 1)
                yield t0 + 6 + k
            yield t0 + 10
            pe.wait_ge(S["gz_sb"], 2)
            pe.wait_ge(S["xm_sb"], 2)
            yield from prep_tensor(pe, 2, 0, S["conv_silu"], 1, t0 + 10)

        def l1_pre_scalar(act, t0):
            act.wait_ge(S["cols_now"], 1)
            act.wait_ge(S["xt_full_b"], 1)
            for d in range(DB):
                last = nc.scalar.activation(xT[:, d, :], bank(0, DB)[:, d, :], ACT.Identity, scale=cols1[:, d:d + 1],
                                            bias=cols1[:, DB + d:DB + d + 1])
            last.then_inc(S["xt_sb_b"], 1)
            yield t0 + 9
            for k in range(2):
                act.wait_ge(S["gz_full"], k + 1)
                nc.scalar.activation(act_z[:, 2 * k:2 * k + 2, :], bank(k, 2), ACT.Silu).then_inc(S["gz_sb"], 1)
                yield t0 + 9
            act.wait_ge(S["conv_done"], (CT - 1) * EB)
            nc.scalar.activation(u_s[2][:, :, :], acc[:, :, :], ACT.Silu).then_inc(S["conv_silu"], 1)
            yield t0 + 12
            yield from prep_scalar(act, 2, 0, t0 + 10)

        def l1_post_tensor(pe, t0):
            for k in range(2):
                for j in range(2):
                    eb = 2 * k + j
                    for t in range(TB):
                        last = nc.tensor.matmul(bank(k, 2)[:, j, t * P:(t + 1) * P], yt[2][:, t, eb * P:(eb + 1) * P],
                                                ident[:, :], is_transpose=True, start=True, stop=True)
                last.then_inc(S["yb_full_1"], 1)
            yield t0 + 2
            pe.wait_ge(S["yg_1"], 2)
            for t in range(TB):
                last = to_tokens(bank(2, TB)[:, t, :], yg, t, w["wout1"], EB)
                if t == 0:
                    yield t0 + 3
            last.then_inc(S["o_full_1"], 1)
            yield t0 + 5
            pe.wait_ge(S["o_sb_1"], 1)
            for q in range(TB):
                for t in range(TB):
                    last = nc.tensor.matmul(bank(0, TB)[:, q, :], gath[:, t, q * P:(q + 1) * P], tmp[:, t, :],
                                            start=(t == 0), stop=(t == TB - 1))
            last.then_inc(S["og_full_1"], 1)
            yield t0 + 7
            pe.wait_ge(S["res_1"], 1)
            yield t0 + 7

        def l1_post_scalar(act, t0):
            act.wait_ge(S["o_full_1"], 1)
            nc.scalar.activation(tmp[:, :, :], bank(2, TB), ACT.Copy).then_inc(S["o_sb_1"], 1)
            yield t0 + 5

        def l1_post_vector(dve, ch, t0):
            for k in range(2):
                dve.wait_ge(S["yb_full_1"], k + 1)
                nc.vector.tensor_tensor(yg[:, 2 * k:2 * k + 2, :], bank(k, 2), act_z[:, 2 * k:2 * k + 2, :],
                                        ALU.mult).then_inc(S["yg_1"], 1)
            yield t0 + 6
            dve.wait_ge(S["gate_in"], 16)
            dve.wait_ge(S["og_full_1"], 1)
            ch.done(nc.vector.tensor_tensor(x2[:, :, :], bank(0, TB), gate1[:, :].unsqueeze(1).broadcast_to([P, TB, D]),
                                            ALU.mult))
            nc.vector.tensor_tensor(x2[:, :, :], x2[:, :, :], xr[:, :, :], ALU.add).then_inc(S["res_1"], 1)
            dve.wait_ge(S["res_1"], 1)
            yield t0 + 7

        def l1_post_sync(sp, b):
            sp.dma_start(gate1[:, :], mod_rows[bass.ds(b, 1), 3 * D:4 * D].rearrange("b d -> (b d)")
                         .partition_broadcast(P)).then_inc(S["gate_in"], 16)

        def tail_tensor(pe, weight, bias, yn, yt_full, yt_sb, h_full, res, t0):
            pe.wait_ge(yn, 1)
            turn(xn, 0, yt_full)
            yield t0 + 3
            pe.wait_ge(yt_sb, 1)
            for t in range(TB):
                last = to_tokens(bank(1, TB)[:, t, :], xT, t, weight, DB, bias)
            last.then_inc(h_full, 1)
            yield t0 + 5
            pe.wait_ge(res, 1)
            yield t0 + 5

        def tail_scalar(act, k, yt_full, yt_sb, t0):
            act.wait_ge(yt_full, 1)
            for d in range(DB):
                last = nc.scalar.activation(xT[:, d, :], bank(0, DB)[:, d, :], ACT.Silu,
                                            scale=cols23[:, k * DB + d:k * DB + d + 1],
                                            bias=cols23[:, (k + 1) * DB + d:(k + 1) * DB + d + 1])
            last.then_inc(yt_sb, 1)
            yield t0 + 3

        def tail_vector(dve, ch, slot, yn, h_full, res, t0):
            norm(ch, slot, yv, plain(yv)).then_inc(yn, 1)
            yield t0 + 4
            dve.wait_ge(h_full, 1)
            nc.vector.tensor_tensor(x2[:, :, :], bank(1, TB), x2[:, :, :], ALU.add).then_inc(res, 1)
            dve.wait_ge(res, 1)
            yield t0 + 5

        def l2_tensor(pe, t0):
            pe.wait_ge(S["xn_c"], 1)
            turn(xn, 0, S["xt_full_c"])
            yield t0 + 3
            pe.wait_ge(S["xt_sb_c"], 1)
            for k in range(4):
                if k >= 2:
                    pe.wait_ge(S["q_sb"], k - 1)
                for j in range(2):
                    last = project(bank(1 + k % 2, 2)[:, j, :], (w["wq2"], w["wk2"])[k // 2], (2 * (k % 2) + j) * P, P, xT, DB)
                last.then_inc(S["qk_full"], 1)
                yield t0 + 4 + k
            for t in range(TB):
                last = to_tokens(bank(0, TB)[:, t, :], xT, t, w["wv2"], DB, "bv2")
            last.then_inc(S["v2_full"], 1)
            yield t0 + 9
            pe.wait_ge(S["v2_sb"], 1)
            pe.wait_ge(S["q_sb"], 2)
            pe.wait_ge(S["k_sb"], 4)
            for h in range(H2 + 3):
                if h < H2:
                    if h >= 1:
                        pe.wait_ge(S["s_max"], h)
                    r, hb = 32 * (h % HPB), h // HPB
                    for q in range(TB):
                        last = nc.tensor.matmul(bank(0, TB)[:, q, :], qT[r:r + DH2 + 1, hb, q * P:(q + 1) * P],
                                                kT[r:r + DH2 + 1, hb, :], start=True, stop=True)
                    last.then_inc(S["s_full"], 1)
                if 2 <= h < H2 + 2:
                    v = h - 2
                    pe.wait_ge(S["p_ready"], v + 1)
                    if v >= 1:
                        pe.wait_ge(S["pt_sb"], v)
                    for m in range(TB):
                        for q in range(TB):
                            last = nc.tensor.matmul(bank(1, TB)[:, m, q * P:(q + 1) * P],
                                                    pr[:, v % 2, q, m * P:(m + 1) * P], ident[:, :],
                                                    is_transpose=True, start=True, stop=True)
                    last.then_inc(S["pt_full"], 1)
                if h >= 3:
                    v = h - 3
                    pe.wait_ge(S["pt_sb"], v + 1)
                    if v == H2 // 2:
                        pe.wait_ge(S["o_taken_2"], 1)
                    o = bank(2, TB).rearrange("p q (h l) -> p q h l", l=32)[:, :, v % 8, 0:DH2 + 1]
                    for q in range(TB):
                        for m in range(TB):
                            last = nc.tensor.matmul(o[:, q, :], pT[:, v % 2, m, q * P:(q + 1) * P], v2[:, m, v, :],
                                                    start=(m == 0 and q == 0 and v % 8 == 0), stop=(m == TB - 1),
                                                    skip_group_check=True)
                    last.then_inc(S["o_full_2"], 1)
                yield t0 + 10 + h
            pe.wait_ge(S["o_taken_2"], 2)
            yield from tail_tensor(pe, w["wo2"], "bo2", S["yn_2"], S["yt_full_2"], S["yt_sb_2"], S["h_full_2"], S["res_2"], t0 + 27)

        def l2_scalar(act, t0):
            act.wait_ge(S["xt_full_c"], 1)
            for d in range(DB):
                last = nc.scalar.activation(xT[:, d, :], bank(0, DB)[:, d, :], ACT.Identity, scale=c["l2w"][:, d:d + 1],
                                            bias=c["l2b"][:, d:d + 1])
            last.then_inc(S["xt_sb_c"], 1)
            yield t0 + 4
            for k in range(2):
                act.wait_ge(S["qk_full"], k + 1)
                for j in range(2):
                    hb = 2 * k + j
                    last = nc.scalar.activation(qT[:, hb, :], bank(1 + k, 2)[:, j, :], ACT.Identity,
                                                bias=c["bq2"][:, hb:hb + 1])
                last.then_inc(S["q_sb"], 1)
                yield t0 + 5 + k
            yield t0 + 8
            act.wait_ge(S["v2_full"], 1)
            for t in range(TB):
                last = nc.scalar.activation(v2[:, t, :, 0:DH2], bank(0, TB)[:, t, :].rearrange("p (h l) -> p h l", l=DH2),
                                            ACT.Copy, scale=masks[:, t:t + 1])
            last.then_inc(S["v2_sb"], 1)
            yield t0 + 10
            for h in range(H2):
                act.wait_ge(S["s_max"], h + 1)
                if h >= 2:
                    act.wait_ge(S["pt_full"], h - 1)
                for q in range(TB):
                    last = nc.scalar.activation(pr[:, h % 2, q, :], sc_s[:, h % 2, q, :], ACT.Exp,
                                                bias=mx[:, h % 2, 1, q:q + 1])
                last.then_inc(S["p_ready"], 1)
                if h >= 1:
                    self_copy(act, h - 1)
                yield t0 + 11 + h
            self_copy(act, H2 - 1)
            yield t0 + 29
            yield from tail_scalar(act, 0, S["yt_full_2"], S["yt_sb_2"], t0 + 27)

        def self_copy(act, v):
            act.wait_ge(S["pt_full"], v + 1)
            if v >= 2:
                act.wait_ge(S["o_full_2"], v - 1)
            nc.scalar.activation(pT[:, v % 2, :, :], bank(1, TB), ACT.Copy).then_inc(S["pt_sb"], 1)

        def l2_vector(dve, ch, b, t0):
            ch.done(nc.vector.tensor_copy(cols23[:, :].unsqueeze(2), mod_cols[:, 2 * DB:6 * DB, bass.ds(b, 1)]))
            ch.done(nc.vector.tensor_copy(masks[:, 0:TB], c["mask2"][:, bass.ds(b * TB, TB)]))
            ch.done(nc.vector.tensor_copy(masks[:, TB:2 * TB], c["mask3"][:, bass.ds(b * TB, TB)]))
            ch.done(nc.vector.memset(v2[:, :, :, DH2:DH2 + 1], 1.0))
            norm(ch, 3, x2, plain(x2)).then_inc(S["xn_c"], 1)
            yield t0 + 6
            dve.wait_ge(S["key_in"], 16)
            ch.done(nc.vector.tensor_scalar(keymask[:, :], keymask[:, :], 1.0, c["keyrow"][:, 0:1], ALU.subtract, ALU.mult))
            for k in range(2):
                dve.wait_ge(S["qk_full"], 3 + k)
                for j in range(2):
                    hb = 2 * k + j
                    nc.vector.scalar_tensor_tensor(out=kT[:, hb, :], in0=bank(1 + k, 2)[:, j, :],
                                                   scalar=c["bk2"][:, hb:hb + 1], in1=keymask[:, :], op0=ALU.add,
                                                   op1=ALU.add).then_inc(S["k_sb"], 1)
                yield t0 + 7 + k
            yield t0 + 9
            for h in range(H2):
                dve.wait_ge(S["s_full"], h + 1)
                if h >= 2:
                    dve.wait_ge(S["p_ready"], h - 1)
                for q in range(TB):
                    last = ch.mark(nc.vector.tensor_scalar(sc_s[:, h % 2, q, :], bank(0, TB)[:, q, :],
                                                           0.0, None, ALU.add, ALU.max,
                                                           accum_out=mx[:, h % 2, 0, q:q + 1]))
                dve.wait_ge(S["dve_chain"], last)
                nc.vector.tensor_scalar(mx[:, h % 2, 1, :], mx[:, h % 2, 0, :], -1.0, None, ALU.mult).then_inc(S["s_max"], 1)
                if h == H2 // 2 + 2:
                    take_heads(dve, ch, 0)
                yield t0 + 10 + h
            yield t0 + 27
            take_heads(dve, ch, 1)
            yield from tail_vector(dve, ch, 0, S["yn_2"], S["h_full_2"], S["res_2"], t0 + 27)

        def take_heads(dve, ch, half):
            dve.wait_ge(S["o_full_2"], (half + 1) * H2 // 2)
            o = bank(2, TB).rearrange("p q (h l) -> p q h l", l=32)
            for q in range(TB):
                last = ch.mark(nc.vector.reciprocal(rec[:, half, q, :].unsqueeze(2), o[:, q, :, DH2:DH2 + 1]))
            dve.wait_ge(S["dve_chain"], last)
            for q in range(TB):
                last = ch.mark(nc.vector.tensor_tensor(
                    yv[:, q, half * P:(half + 1) * P].rearrange("p (h l) -> p h l", l=DH2), o[:, q, :, 0:DH2],
                    rec[:, half, q, :].unsqueeze(2).broadcast_to([P, H2 // 2, DH2]), ALU.mult))
            dve.wait_ge(S["dve_chain"], last)
            nc.vector.engine_nop().then_inc(S["o_taken_2"], 1)

        def l3_tensor(pe, t0):
            pe.wait_ge(S["xn_d"], 1)
            turn(xn, 0, S["xt_full_d"])
            yield t0 + 3
            pe.wait_ge(S["xt_sb_d"], 1)
            for t in range(TB):
                last = to_tokens(bank(1, TB)[:, t, :], xT, t, w["wq3"], DB, "bq3")
            last.then_inc(S["qkv_full"], 1)
            yield t0 + 4
            for d in range(DB):
                last = project(bank(2, DB)[:, d, :], w["wk3"], d * P, P, xT, DB)
            last.then_inc(S["qkv_full"], 1)
            yield t0 + 5
            for t in range(TB):
                last = to_tokens(bank(0, TB)[:, t, :], xT, t, w["wv3"], DB, "bv3")
            last.then_inc(S["qkv_full"], 1)
            yield t0 + 7
            pe.wait_ge(S["q_exp"], 1)
            turn(pr[:, 0, :, :], 1, S["qk3_t"])
            pe.wait_ge(S["k_exp"], DB)
            for t in range(TB):
                for d in range(DB):
                    last = nc.tensor.matmul(bank(2, TB)[:, t, d * P:(d + 1) * P], pr[:, 1, d, t * P:(t + 1) * P],
                                            ident[:, :], is_transpose=True, start=True, stop=True)
            last.then_inc(S["qk3_t"], 1)
            yield t0 + 9
            pe.wait_ge(S["qk3_sb"], 2)
            pe.wait_ge(S["v3_sb"], 1)
            for d in range(DB):
                for t in range(TB):
                    last = nc.tensor.matmul(bank(0)[:, d * P:(d + 1) * P], pT[:, 1, t, d * P:(d + 1) * P],
                                            tmp3[:, t, d * P:(d + 1) * P], start=(t == 0), stop=(t == TB - 1))
            last.then_inc(S["bd_full"], 1)
            yield t0 + 11
            pe.wait_ge(S["bd_sb"], DB)
            for t in range(TB):
                for d in range(DB):
                    last = nc.tensor.matmul(bank(1, TB)[:, t, d * P:(d + 1) * P], pT[:, 0, d, t * P:(t + 1) * P],
                                            bd[:, d, :], start=True, stop=True)
            last.then_inc(S["y3_full"], 1)
            yield t0 + 13
            yield from tail_tensor(pe, w["wo3"], "bo3", S["yn_3"], S["yt_full_3"], S["yt_sb_3"], S["h_full_3"], S["res_3"], t0 + 12)

        def l3_scalar(act, t0):
            act.wait_ge(S["xt_full_d"], 1)
            for d in range(DB):
                last = nc.scalar.activation(xT[:, d, :], bank(0, DB)[:, d, :], ACT.Identity, scale=c["l3w"][:, d:d + 1],
                                            bias=c["l3b"][:, d:d + 1])
            last.then_inc(S["xt_sb_d"], 1)
            yield t0 + 6
            act.wait_ge(S["qkv_full"], 3)
            for t in range(TB):
                last = nc.scalar.activation(tmp3[:, t, :], bank(0, TB)[:, t, :], ACT.Copy, scale=masks[:, TB + t:TB + t + 1])
            last.then_inc(S["v3_sb"], 1)
            act.wait_ge(S["q_sub"], 1)
            nc.scalar.activation(pr[:, 0, :, :], sc_s[:, 0, :, :], ACT.Exp).then_inc(S["q_exp"], 1)
            act.wait_ge(S["k_sub"], 1)
            for d in range(DB):
                nc.scalar.activation(pr[:, 1, d, :], sc_s[:, 1, d, :], ACT.Exp, bias=kmax[:, 1, d:d + 1],
                                     accum_out=kmax[:, 2, d:d + 1]).then_inc(S["k_exp"], 1)
            yield t0 + 8
            for k in range(2):
                act.wait_ge(S["qk3_t"], k + 1)
                nc.scalar.activation(pT[:, k, :, :], bank(1 + k, 2), ACT.Copy).then_inc(S["qk3_sb"], 1)
            yield t0 + 14
            yield from tail_scalar(act, 2, S["yt_full_3"], S["yt_sb_3"], t0 + 12)

        def l3_vector(dve, ch, t0):
            dve.wait_ge(S["mask_in"], 16)
            ch.done(nc.vector.tensor_scalar(maskrow[:, :], maskrow[:, :], 1.0, NEG, ALU.subtract, ALU.mult))
            norm(ch, 1, x2, plain(x2)).then_inc(S["xn_d"], 1)
            yield t0 + 4
            dve.wait_ge(S["qkv_full"], 1)
            q = bank(1).rearrange("p (g l) -> p g l", l=DH3)
            ch.done(nc.vector.tensor_reduce(r3[:, 0, :], q, AX.X, ALU.max))
            nc.vector.tensor_tensor(sc_s[:, 0, :, :].rearrange("p t (h l) -> p (t h) l", l=DH3), q,
                                    r3[:, 0, :].unsqueeze(2).broadcast_to([P, TB * H3, DH3]),
                                    ALU.subtract).then_inc(S["q_sub"], 1)
            yield t0 + 5
            dve.wait_ge(S["qkv_full"], 2)
            for d in range(DB):
                last = ch.mark(nc.vector.scalar_tensor_tensor(
                    out=sc_s[:, 1, d, :], in0=bank(2, DB)[:, d, :], scalar=c["bk3"][:, d:d + 1], in1=maskrow[:, :],
                    op0=ALU.add, op1=ALU.add))
            dve.wait_ge(S["dve_chain"], last)
            ch.done(nc.vector.tensor_reduce(kmax[:, 0, :], sc_s[:, 1, :, :], AX.X, ALU.max))
            nc.vector.tensor_scalar(kmax[:, 1, :], kmax[:, 0, :], -1.0, None, ALU.mult).then_inc(S["k_sub"], 1)
            yield t0 + 7
            dve.wait_ge(S["q_exp"], 1)
            ch.done(nc.vector.tensor_reduce(r3[:, 1, :], pr[:, 0, :, :].rearrange("p t (h l) -> p (t h) l", l=DH3),
                                            AX.X, ALU.add))
            ch.mark(nc.vector.reciprocal(r3[:, 2, :], r3[:, 1, :]))
            dve.wait_ge(S["k_exp"], DB)
            ch.done(nc.vector.reciprocal(kmax[:, 3, :], kmax[:, 2, :]))
            yield t0 + 10
            dve.wait_ge(S["bd_full"], 1)
            for d in range(DB):
                nc.vector.scalar_tensor_tensor(out=bd[:, d, :], in0=bank(0)[:, d * P:(d + 1) * P],
                                               scalar=kmax[:, 3, d:d + 1], in1=blockmask[:, :], op0=ALU.mult,
                                               op1=ALU.mult).then_inc(S["bd_sb"], 1)
            yield t0 + 12
            dve.wait_ge(S["y3_full"], 1)
            ch.done(nc.vector.tensor_tensor(yv[:, :, :].rearrange("p t (h l) -> p (t h) l", l=DH3),
                                            bank(1).rearrange("p (g l) -> p g l", l=DH3),
                                            r3[:, 2, :].unsqueeze(2).broadcast_to([P, TB * H3, DH3]), ALU.mult))
            yield t0 + 12
            yield from tail_vector(dve, ch, 2, S["yn_3"], S["h_full_3"], S["res_3"], t0 + 12)

        def l2_sync(sp, b):
            sp.dma_start(keymask[:, :], dram["mask2"][bass.ds(b, 1), :].rearrange("b d -> (b d)")
                         .partition_broadcast(P)).then_inc(S["key_in"], 16)

        def l3_sync(sp, b):
            sp.dma_start(maskrow[:, :], dram["mask3"][bass.ds(b, 1), :].rearrange("b d -> (b d)")
                         .partition_broadcast(P)).then_inc(S["mask_in"], 16)

        tmp3 = tmp
        act_chain = [None]

        STAGES = dict(l0_post=(5, 0, 0, 1), l0_pre=(25, 3, 4, 0), l1_post=(7, 0, 4, 1), l1_pre=(19, 1, 2, 0),
                      l2=(32, 1, 2, 0), l3=(17, 1, 2, 0))
        TENSOR, SCALAR, VECTOR = 1, 2, 3

        def run(scan, stages):
            starts, ticks = [], 0
            for name, _ in stages:
                starts.append(ticks)
                ticks += STAGES[name][0]
            per_unit = max(1.0, ticks / UNITS)

            def pieces(table, engine):
                for (name, b), t0 in zip(stages, starts):
                    if name in table:
                        yield t0 + STAGES[name][engine]
                        yield from table[name](b, t0)

            def ticker(gen):
                state = [0, next(gen, None)]

                def tick():
                    state[0] += 1
                    while state[1] is not None and state[1] < int(state[0] * per_unit):
                        state[1] = next(gen, None)
                return tick

            with nc.Block() as block:
                @block.sync
                def _(sp):
                    names = [name for name, _ in stages]
                    for name, b in stages:
                        if name == "l1_post":
                            l1_post_sync(sp, b)
                            sp.wait_ge(S["gate_in"], 16)
                        if name == "l2":
                            l2_sync(sp, b)
                            sp.wait_ge(S["key_in"], 16)
                        if name == "l3":
                            l3_sync(sp, b)
                    for name, b in stages:
                        if name == "l0_pre":
                            if "l0_post" in names:
                                sp.wait_ge(S["res_0"], 1)
                            l0_pre_sync(sp, b)
                    for name, b in stages:
                        if name == "l3":
                            sp.wait_ge(S["mask_in"], 16)
                            sp.wait_ge(S["res_3"], 1)
                            sp.dma_start(out[bass.ds(b, 1)].rearrange("b (k p) d -> p (b k) d", p=P),
                                         x2[:, :, :]).then_inc(S["out_done"], 16)
                            sp.wait_ge(S["out_done"], 16)
                    if "l0_pre" in names:
                        sp.wait_ge(S["x_in"], 16)
                        sp.wait_ge(S["row_in"], 16)

                @block.tensor
                def _(pe):
                    gen = pieces({"l0_post": lambda b, t0: l0_post_tensor(pe, t0), "l0_pre": lambda b, t0: l0_pre_tensor(pe, t0),
                                  "l1_post": lambda b, t0: l1_post_tensor(pe, t0), "l1_pre": lambda b, t0: l1_pre_tensor(pe, t0),
                                  "l2": lambda b, t0: l2_tensor(pe, t0), "l3": lambda b, t0: l3_tensor(pe, t0)}, TENSOR)
                    if scan:
                        scan.tensor(pe, ticker(gen))
                    for _ in gen:
                        pass

                @block.scalar
                def _(act):
                    act_chain[0] = Chain(act, S["act_chain"])
                    gen = pieces({"l0_pre": lambda b, t0: l0_pre_scalar(act, t0), "l1_post": lambda b, t0: l1_post_scalar(act, t0),
                                  "l1_pre": lambda b, t0: l1_pre_scalar(act, t0), "l2": lambda b, t0: l2_scalar(act, t0),
                                  "l3": lambda b, t0: l3_scalar(act, t0)}, SCALAR)
                    if scan:
                        scan.scalar(act, ticker(gen))
                    for _ in gen:
                        pass

                @block.vector
                def _(dve):
                    ch = Chain(dve, S["dve_chain"])
                    gen = pieces({"l0_post": lambda b, t0: l0_post_vector(dve, ch, t0), "l0_pre": lambda b, t0: l0_pre_vector(dve, ch, t0),
                                  "l1_post": lambda b, t0: l1_post_vector(dve, ch, t0), "l1_pre": lambda b, t0: l1_pre_vector(dve, ch, b, t0),
                                  "l2": lambda b, t0: l2_vector(dve, ch, b, t0), "l3": lambda b, t0: l3_vector(dve, ch, t0)}, VECTOR)
                    if scan:
                        scan.vector(dve, ticker(gen))
                    for _ in gen:
                        pass

                if scan:
                    @block.gpsimd
                    def _(pool):
                        scan.gpsimd(pool)
            nc.multi_engine_barrier(list(mybir.ALL_ENGINES), sems_to_clear=all_sems)

        def iteration(i, first=False, second=False, last=0):
            a = last == 0
            run(Scan(0) if a else None,
                ([] if first or second else [("l1_post", i - 2)]) + ([] if first or last > 1 else [("l1_pre", i - 1)]))
            run(Scan(1, True) if a else None, [] if first or second else [("l2", i - 2)])
            run(Scan(2) if not first and last < 2 else None,
                ([("l0_post", i)] if a else []) + ([] if first or second else [("l3", i - 2)])
                + ([("l0_pre", i + 1)] if a and not (isinstance(i, int) and i == B - 1) else []))

        run(None, [("l0_pre", 0)])
        iteration(0, first=True)
        iteration(1, second=True)
        with nc.Fori(2, B - 1) as i:
            iteration(i)
        iteration(B - 1)
        iteration(B, last=1)
        iteration(B + 1, last=2)


def pack(inputs):
    f = {k: np.asarray(v) for k, v in inputs.items()}

    def blocks(m):
        k, n = m.shape
        return m.reshape(k // P, P, n).transpose(1, 0, 2).reshape(P, -1)

    def spread(m):
        k = m.shape[0]
        out = np.zeros((k, H2, 32), m.dtype)
        out[:, :, :DH2] = m.reshape(k, H2, DH2)
        return out.reshape(k, H2 * 32)

    def column(v):
        return v.reshape(-1, P).T

    def states(m):
        return m.reshape(EB, P, -1).transpose(1, 0, 2).reshape(P, -1)

    key_row = np.zeros(H2 * 32, np.float32)
    key_row[DH2::32] = 1
    L0, L1, L2, L3 = ("L0_cond_", "L1_cond_", "L2_cond_", "L3_cond_")
    ws = dict(wx=f[L0 + "Wx"].T, wf=f[L0 + "Wf"].T,
              wdlt0=f[L0 + "Wdbc1"][:R].T, wbc0=f[L0 + "Wdbc1"][R:].T,
              wdlt1=f[L0 + "Wdbc2"][:R].T, wbc1=f[L0 + "Wdbc2"][R:].T,
              win=f[L1 + "W_in"], wdlt2=f[L1 + "W_xp"][:, :R], wbc2=f[L1 + "W_xp"][:, R:], wout1=f[L1 + "W_out"],
              wq2=spread(f[L2 + "q_w"]), wk2=spread(f[L2 + "k_w"]), wv2=f[L2 + "v_w"], wo2=f[L2 + "out_w"],
              wq3=f[L3 + "Wq"], wk3=f[L3 + "Wk"], wv3=f[L3 + "Wv"], wo3=f[L3 + "W_out"])
    cs = dict(n2g=column(f[L0 + "norm2_g"]), n2b=column(f[L0 + "norm2_b"]), bx=column(f[L0 + "bx"]),
              bz=column(f[L0 + "bz"]), bc0=column(f[L0 + "bc1"]), bc1=column(f[L0 + "bc2"]),
              bdt0=column(f[L0 + "bdt1"]), bdt1=column(f[L0 + "bdt2"]), bdt2=column(f[L1 + "b_dt"]),
              dp0=column(f[L0 + "Dp1"]), dp1=column(f[L0 + "Dp2"]), dp2=column(f[L1 + "D_param"]),
              alog0=states(f[L0 + "Alog1"]), alog1=states(f[L0 + "Alog2"]), alog2=states(f[L1 + "A_log"]),
              convw=states(f[L1 + "conv_w"].reshape(E, CT)), convb=column(f[L1 + "conv_b"]),
              l2w=column(f[L2 + "norm_w"]), l2b=column(f[L2 + "norm_b"]),
              bq2=column(spread(f[L2 + "q_b"][None])[0] + key_row), bk2=column(spread(f[L2 + "k_b"][None])[0]),
              l3w=column(f[L3 + "ln_w"]), l3b=column(f[L3 + "ln_b"]), bk3=column(f[L3 + "bk"]),
              mask2=column(f["mask_BxS_ff1"].reshape(-1)), mask3=column(f["mask_BxSx1_fk1"].reshape(-1)),
              keyrow=(NEG * key_row[:P])[:, None])
    return {
        "x": f["x"],
        "weights": np.concatenate([blocks(ws[k]) for k in WEIGHTS], 1),
        "columns": np.concatenate([cs[k] for k in COLUMNS], 1),
        "wdt": np.stack([f[L0 + "Wdt1"].T, f[L0 + "Wdt2"].T, f[L1 + "W_dt"]], 1),
        "bias_rows": np.stack([f[L0 + "bf"], f[L2 + "v_b"], f[L2 + "out_b"], f[L3 + "bq"], f[L3 + "bv"],
                               f[L3 + "b_out"]])[None],
        "ada_w": blocks(np.concatenate([f[L0 + "Wada"].T, f[L1 + "W_ada"], f[L2 + "emb_w"], f[L3 + "W_emb"]], 1))
        .reshape(P, CB_, NADA),
        "ada_b": np.concatenate([f[L0 + "bada"], f[L1 + "b_ada"], f[L2 + "emb_b"], f[L3 + "b_emb"]])[None],
        "cond": f["cond_2048"].T.reshape(CB_, P, B).transpose(1, 0, 2),
        "norm_rows": np.stack([f[L0 + "norm1_g"], f[L0 + "norm1_b"], f[L1 + "gamma"], f[L1 + "beta"],
                               f[L2 + "sb_norm_w"], f[L2 + "sb_norm_b"], f[L3 + "ln2_w"], f[L3 + "ln2_b"]]),
        "wz": blocks(f[L0 + "Wz"]).reshape(P, EB, D),
        "wc": np.stack([blocks(f[L0 + "Wc1"].T).reshape(P, EB, E), blocks(f[L0 + "Wc2"].T).reshape(P, EB, E)], 1),
        "itok": f["itok_S_0_1023"],
        "mask2": f["mask_BxS_ff1"],
        "mask3": f["mask_BxSx1_fk1"].reshape(B, T),
    }


def kernel(**inputs):
    import concourse.bacc as _bacc
    from concourse.bass_utils import run_bass_kernel_spmd as _run

    nc = _bacc.Bacc("TRN2", target_bir_lowering=False, num_devices=1)
    arrays, dram = {}, {}
    for name, a in pack(inputs).items():
        a = np.ascontiguousarray(a)
        arrays[f"in_{name}_dram"] = a
        dram[name] = nc.dram_tensor(f"in_{name}_dram", a.shape, mybir.dt.from_np(a.dtype), kind="ExternalInput").ap()
    out = nc.dram_tensor("out_0_dram", (B, T, D), F32, kind="ExternalOutput").ap()
    build(nc, dram, out)
    r = _run(nc, [arrays], core_ids=[0])
    return r.results[0]["out_0_dram"]
```

```python
from contextlib import ExitStack

import numpy as np

import concourse.bass as bass
from concourse import mybir

F32 = mybir.dt.float32
I32 = mybir.dt.int32
ALU = mybir.AluOpType
ACT = mybir.ActivationFunctionType
AX = mybir.AxisListType

P = 128
B, T, D = 16, 256, 256
E, N, R = 512, 16, 64
TB, DB, EB = T // P, D // P, E // P
CT = 4
C2 = 2 * D
CB_ = C2 // P
H2, DH2 = 16, D // 16
HPB = 4
H3, DH3 = 8, D // 8
EPS = 1e-5
NEG = 1e6
HALF = EB // 2
UNITS = (EB // HALF) * N
S_BANKS = (0, 3)
PV_LAG = 4
B_AHEAD = 4
DA_AHEAD = 2
LAG = 4
RESET = 1e37
ADAW = [3 * D, 3 * D, 2 * D, 2 * D]
NADA = sum(ADAW)

WEIGHTS = dict(wx=(DB, E), wf=(EB, D), wdlt0=(EB, R), wbc0=(EB, 2 * N), wdlt1=(EB, R), wbc1=(EB, 2 * N),
               win=(DB, 2 * E), wdlt2=(EB, R), wbc2=(EB, 2 * N), wout1=(EB, D),
               wq2=(DB, 4 * P), wk2=(DB, 4 * P), wv2=(DB, D), wo2=(DB, D),
               wq3=(DB, D), wk3=(DB, D), wv3=(DB, D), wo3=(DB, D))
COLUMNS = dict(n2g=DB, n2b=DB, bx=EB, bz=EB, bc0=EB, bc1=EB, bdt0=EB, bdt1=EB, bdt2=EB,
               dp0=EB, dp1=EB, dp2=EB, alog0=EB * N, alog1=EB * N, alog2=EB * N,
               convw=EB * CT, convb=EB, l2w=DB, l2b=DB, bq2=4, bk2=4, l3w=DB, l3b=DB, bk3=DB,
               mask2=B * TB, mask3=B * TB, keyrow=1)
BIASROWS = ["bf", "bv2", "bo2", "bq3", "bv3", "bo3"]
NORMROWS = 8
CHUNK = 4
CHUNKS = N // CHUNK
NDBU, NHST, NG, NSC, NPT = 2, 4, 3, 3, 2


def offsets(widths):
    at, out = 0, {}
    for name, w in widths.items():
        out[name] = (at, w)
        at += w
    return out, at


WOFF, WTOT = offsets({k: a * b for k, (a, b) in WEIGHTS.items()})
COFF, CTOT = offsets(COLUMNS)

SEMS = """
loaded consts cond_act ada_full ada_taken ada_bias rows_ready rows_stored cols_full cols_taken alog_exp alog_done
fold_full fold_taken foldb_full foldb_done gather_ready itok_f
dve_chain act_chain pool_chain
b_full dbu_done c_in_0 c_in_1 c_in_2 c_in_3 da_ready scan_done g_ready g_used y_taken
ct_full ct_sb c_stored prep_done key_in q_sb k_sb
x_in row_in gate_in out_done cols_now
xn_a xt_full_a xt_sb_a mx_full mx_sb z_full z_sb
dlt_full dt_read bc_full bc_sb dt_full sp_clip sp_log
yb_full_0 yg_0 o_full_0 res_0
xn_b xt_full_b xt_sb_b xm_full xm_sb gz_full gz_sb conv_acc conv_done conv_silu
yb_full_1 yg_1 o_full_1 o_sb_1 og_full_1 res_1
xn_c xt_full_c xt_sb_c qk_full v2_full v2_sb s_full s_max p_ready pt_full pt_sb o_full_2 o_taken_2
yn_2 yt_full_2 yt_sb_2 h_full_2 res_2
xn_d xt_full_d xt_sb_d qkv_full v3_sb q_sub q_exp k_sub k_exp qk3_t qk3_sb bd_full bd_sb y3_full yn_3 yt_full_3 yt_sb_3
h_full_3 res_3 mask_in
""".split()


def build(nc, dram, out):
    with ExitStack() as ctx:
        def sb(name, shape, dt=F32):
            return ctx.enter_context(nc.sbuf_tensor(name, shape, dt))

        def ps(name, shape):
            return ctx.enter_context(nc.psum_tensor(name, shape, F32))

        S = {n: ctx.enter_context(nc.semaphore(n)) for n in SEMS}
        sem_nums = [v.num for v in S.values()]
        assert sem_nums == list(range(sem_nums[0], sem_nums[0] + len(SEMS)))
        all_sems = range(sem_nums[0], sem_nums[-1] + 1)

        mod_rows = nc.dram_tensor("mod_rows", (B, 4 * D), F32, kind="Internal").ap()
        c_rows = nc.dram_tensor("c_rows", (3, N, T), F32, kind="Internal").ap()

        W = sb("weights", [P, WTOT])
        w = {k: W[:, WOFF[k][0]:WOFF[k][0] + a * b].rearrange("p (k m) -> p k m", k=a)
             for k, (a, b) in WEIGHTS.items()}
        CO = sb("columns", [P, CTOT])
        c = {k: CO[:, o:o + n] for k, (o, n) in COFF.items()}
        wdt_bias = sb("wdt_bias", [R + 1, 3 * E])
        wdt = wdt_bias[0:R, :].rearrange("p (s e) -> p s e", s=3)
        brow = wdt_bias[R:R + 1, :].rearrange("p (r d) -> p r d", d=D)
        z1w = sb("z1w", [P, DB, E])
        z2w = sb("z2w", [P, DB, E])
        z1b = sb("z1b", [P, EB])
        z2b = sb("z2b", [P, EB])
        acoef = sb("acoef", [P, 3, EB, N])
        mod_cols = sb("mod_cols", [P, 6 * DB, B])
        ident = sb("ident", [P, P])
        ones = sb("ones", [R + 1, P])
        gath = sb("gather", [P, TB, T])
        blockmask = sb("blockmask", [P, P])

        ps_b = ps("ps_b", [P, 2, 512])
        ps_y = ps("ps_y", [P, TB, HALF * P])
        ps_w = ps("ps_w", [P, 4, 512])
        ps_v = ps("ps_v", [P, 512])

        def bank(k, m=None):
            return ps_w[:, k, :] if m is None else ps_w[:, k, :].rearrange("p (a n) -> p a n", a=m)

        pair = ps_v[:, :].rearrange("p (a n) -> p a n", a=2)

        with ExitStack() as pro:
            def sbp(name, shape, dt=F32):
                return pro.enter_context(nc.sbuf_tensor(name, shape, dt))

            ada_w = sbp("ada_w", [P, CB_, NADA])
            ada_b = sbp("ada_b", [1, NADA])
            cond = sbp("cond", [P, CB_, B])
            cond_s = sbp("cond_s", [P, CB_, B])
            norm_rows = sbp("norm_rows", [B, NORMROWS, D])
            mods = sbp("mods", [B, NADA])
            rows = sbp("rows", [B, 10, D])
            scaled = sbp("scaled", [B, 4, D])
            wz = sbp("wz", [P, EB, D])
            wc = sbp("wc", [P, 2, EB, E])
            itok_i = sbp("itok_i", [P, T], I32)
            itok = sbp("itok", [P, T])
            token = sbp("token", [P, TB])

            with nc.Block() as block:
                loads = [(W[:, :], dram["weights"]), (CO[:, :], dram["columns"]),
                         (wdt_bias[:, :], dram["wdt_bias"]),
                         (ada_w[:, :, :], dram["ada_w"]), (ada_b[:, :], dram["ada_b"]),
                         (cond[:, :, :], dram["cond"]),
                         (norm_rows[:, :, :], dram["norm_rows"].partition_broadcast(B)),
                         (wz[:, :, :], dram["wz"]), (wc[:, :, :, :], dram["wc"]),
                         (itok_i[:, :], dram["itok"].partition_broadcast(P))]
                ALL_LOADED = 16 * len(loads)

                @block.sync
                def _(sp):
                    for dst, src in loads:
                        sp.dma_start(dst, src).then_inc(S["loaded"], 16)
                    sp.wait_ge(S["rows_ready"], 1)
                    sp.dma_start(mod_rows, rows[:, 0:4, :].rearrange("b r d -> b (r d)")).then_inc(S["rows_stored"], 16)
                    sp.wait_ge(S["rows_stored"], 16)

                @block.gpsimd
                def _(pool):
                    n = 0

                    def done(ins):
                        nonlocal n
                        n += 1
                        ins.then_inc(S["pool_chain"], 1)
                        pool.wait_ge(S["pool_chain"], n)

                    done(pool.memset(ident[:, :], 0.0))
                    done(pool.affine_select(out=ident[:, :], in_=ident[:, :], compare_op=ALU.not_equal, fill=1.0,
                                            base=0, pattern=[[-1, P]], channel_multiplier=1))
                    done(pool.memset(ones[:, :], 1.0))
                    done(pool.memset(blockmask[:, :], 1.0))
                    by_head = blockmask[:, :].rearrange("p (h l) -> p h l", l=DH3)
                    done(pool.affine_select(out=by_head, in_=by_head, compare_op=ALU.is_ge, fill=0.0, base=0,
                                            pattern=[[-DH3, P // DH3], [0, DH3]], channel_multiplier=1))
                    done(pool.affine_select(out=by_head, in_=by_head, compare_op=ALU.is_ge, fill=0.0, base=DH3 - 1,
                                            pattern=[[DH3, P // DH3], [0, DH3]], channel_multiplier=-1))
                    done(pool.iota(token[:, :], pattern=[[P, TB]], base=0, channel_multiplier=1,
                                   allow_small_or_imprecise_dtypes=True))
                    pool.nop().then_inc(S["consts"], 1)

                @block.scalar
                def _(act):
                    act.wait_ge(S["loaded"], ALL_LOADED)
                    nc.scalar.activation(cond_s[:, :, :], cond[:, :, :], ACT.Silu).then_inc(S["cond_act"], 1)
                    for j in range(NADA // 512):
                        act.wait_ge(S["ada_full"], j + 1)
                        nc.scalar.activation(mods[:, j * 512:(j + 1) * 512], ps_w[0:B, j % 2, :],
                                             ACT.Copy).then_inc(S["ada_taken"], 1)
                    for j, dst in enumerate((z1w, z1w, z2w, z2w)):
                        act.wait_ge(S["fold_full"], j + 1)
                        nc.scalar.activation(dst[:, j % 2, :], ps_w[:, j % 2, :], ACT.Copy).then_inc(S["fold_taken"], 1)
                    for s, a in enumerate((c["alog0"], c["alog1"], c["alog2"])):
                        nc.scalar.activation(acoef[:, s, :, :], a.rearrange("p (e n) -> p e n", n=N),
                                             ACT.Exp).then_inc(S["alog_exp"], 1)

                @block.tensor
                def _(pe):
                    pe.wait_ge(S["loaded"], ALL_LOADED)
                    pe.wait_ge(S["consts"], 1)
                    pe.wait_ge(S["cond_act"], 1)
                    for j in range(NADA // 512):
                        if j >= 2:
                            pe.wait_ge(S["ada_taken"], j - 1)
                        for k in range(CB_):
                            nc.tensor.matmul(ps_w[0:B, j % 2, :], cond_s[:, k, :], ada_w[:, k, j * 512:(j + 1) * 512],
                                             start=(k == 0), stop=False)
                        nc.tensor.matmul(ps_w[0:B, j % 2, :], ones[0:1, 0:B], ada_b[:, j * 512:(j + 1) * 512],
                                         start=False, stop=True).then_inc(S["ada_full"], 1)
                    for j in range(2 * DB):
                        if j == 0:
                            pe.wait_ge(S["ada_taken"], NADA // 512)
                        if j >= 2:
                            pe.wait_ge(S["fold_taken"], j - 1)
                        for k in range(EB):
                            last = nc.tensor.matmul(ps_w[:, j % 2, :], wz[:, k, (j % DB) * P:(j % DB + 1) * P],
                                                    wc[:, j // DB, k, :], start=(k == 0), stop=(k == EB - 1))
                        last.then_inc(S["fold_full"], 1)
                    for s in range(2):
                        for m in range(EB):
                            for k in range(EB):
                                last = nc.tensor.matmul(ps_y[:, 0, s * EB + m:s * EB + m + 1],
                                                        wc[:, s, k, m * P:(m + 1) * P], c["bz"][:, k:k + 1],
                                                        start=(k == 0), stop=(k == EB - 1))
                    last.then_inc(S["foldb_full"], 1)
                    pe.wait_ge(S["rows_ready"], 1)
                    for r in range(6):
                        for d in range(DB):
                            q = r * DB + d
                            last = nc.tensor.matmul(ps_b[:, 0, q * B:(q + 1) * B], rows[:, 4 + r, d * P:(d + 1) * P],
                                                    ident[0:B, 0:B], is_transpose=True, start=True, stop=True)
                    last.then_inc(S["cols_full"], 1)

                @block.vector
                def _(dve):
                    n = 0

                    def done(ins):
                        nonlocal n
                        n += 1
                        ins.then_inc(S["dve_chain"], 1)
                        dve.wait_ge(S["dve_chain"], n)

                    dve.wait_ge(S["loaded"], ALL_LOADED)
                    dve.wait_ge(S["consts"], 1)
                    done(nc.vector.tensor_copy(itok[:, :], itok_i[:, :]))
                    for k in range(TB):
                        nc.vector.tensor_scalar(gath[:, k, :], itok[:, :], token[:, k:k + 1], None,
                                                ALU.is_equal).then_inc(S["gather_ready"], 1)
                    dve.wait_ge(S["ada_taken"], NADA // 512)
                    at = 0
                    where = []
                    for width in ADAW:
                        where.append(at)
                        at += width
                    for layer, (lo, dst) in enumerate(zip(where, (0, 4, 6, 8))):
                        sc = lo + (D if layer < 2 else 0)
                        sh = lo + (0 if layer < 2 else D)
                        gain, shift = norm_rows[:, 2 * layer, :], norm_rows[:, 2 * layer + 1, :]
                        nc.vector.scalar_tensor_tensor(out=rows[:, dst, :], in0=mods[:, sc:sc + D], scalar=1.0,
                                                       in1=gain, op0=ALU.add, op1=ALU.mult)
                        done(nc.vector.scalar_tensor_tensor(out=scaled[:, layer, :], in0=mods[:, sc:sc + D], scalar=1.0,
                                                            in1=shift, op0=ALU.add, op1=ALU.mult))
                        done(nc.vector.tensor_tensor(rows[:, dst + 1, :], scaled[:, layer, :], mods[:, sh:sh + D],
                                                     ALU.add))
                    for layer in range(2):
                        done(nc.vector.tensor_copy(rows[:, 2 + layer, :],
                                                   mods[:, where[layer] + 2 * D:where[layer] + 3 * D]))
                    nc.vector.engine_nop().then_inc(S["rows_ready"], 1)
                    dve.wait_ge(S["foldb_full"], 1)
                    nc.vector.tensor_tensor(z1b[:, :], ps_y[:, 0, 0:EB], c["bc0"], ALU.add)
                    nc.vector.tensor_tensor(z2b[:, :], ps_y[:, 0, EB:2 * EB], c["bc1"], ALU.add).then_inc(S["foldb_done"], 1)
                    dve.wait_ge(S["cols_full"], 1)
                    nc.vector.tensor_copy(mod_cols[:, :, :].rearrange("p q b -> p (q b)"),
                                          ps_b[:, 0, 0:6 * DB * B]).then_inc(S["cols_taken"], 1)
                    dve.wait_ge(S["alog_exp"], 3)
                    a = acoef[:, :, :, :].rearrange("p s e n -> p (s e n)")
                    nc.vector.tensor_scalar(a, a, -1.0, None, ALU.mult).then_inc(S["alog_done"], 1)
                    dve.wait_ge(S["gather_ready"], TB)
                    dve.wait_ge(S["foldb_done"], 1)
                    dve.wait_ge(S["cols_taken"], 1)
                    dve.wait_ge(S["alog_done"], 1)
                    dve.wait_ge(S["fold_taken"], 4)
            nc.multi_engine_barrier(list(mybir.ALL_ENGINES), sems_to_clear=all_sems)

        u_s = [sb(f"u{s}", [P, EB, T]) for s in range(3)]
        delta = [sb(f"delta{s}", [P, EB, T]) for s in range(3)]
        du = [sb(f"du{s}", [P, EB, T]) for s in range(3)]
        bcm = [sb(f"bcm{s}", [P, TB, 2 * N]) for s in range(3)]
        c_bc = sb("c_bc", [P, N, T])
        decay = sb("decay", [P, DA_AHEAD + 2, HALF, T])
        dbu = sb("dbu", [P, NDBU, 2, HALF, T])
        hst = sb("hst", [P, NHST, HALF, T])
        g = sb("g", [P, NG, HALF, T])
        yt = [u[:, :, :].rearrange("p e t -> p (e t)").rearrange("p (h t c) -> p h t c", h=2, t=TB) for u in u_s]
        x0 = sb("x0", [P, TB, D])
        x1 = sb("x1", [P, TB, D])
        xr = sb("xr", [P, TB, D])
        x2 = sb("x2", [P, TB, D])
        xn = sb("xn", [P, TB, D])
        xT = sb("xT", [P, DB, T])
        rows_bc = sb("rows_bc", [P, 3, D])
        gate1 = sb("gate1", [P, D])
        act_x = sb("act_x", [P, EB, T])
        act_z = sb("act_z", [P, EB, T])
        yg = sb("yg", [P, EB, T])
        xm = sb("xm", [P, EB, CT - 1 + T])
        acc = yg
        xa = yg[:, :, :].rearrange("p e t -> p (e t)")[:, 0:TB * D].rearrange("p (t d) -> p t d", t=TB)
        soft = xm[:, :, 0:T]
        tmp = xn
        ct = xn[0:N, 0, :]
        dlt = xn[0:R, 1, :]
        cols1 = sb("cols1", [P, 2 * DB])
        cols23 = sb("cols23", [P, 4 * DB])
        masks = sb("masks", [P, 2 * TB])
        st = sb("stats", [P, 4, TB, 6])
        mv = sb("mv", [P, 4, TB, 2])
        nrm = sb("nrm", [P, 4, 6, TB])
        xT_x = sb("xT_x", [P, DB, T])
        qT = sb("qT", [P, EB, T])
        kT = sb("kT", [P, EB, T])
        v2 = sb("v2", [P, TB, H2, DH2 + 1])
        pr = sb("pr", [P, NSC, TB, T])
        mx = sb("mx", [P, 2, 2, TB])
        pT = sb("pT", [P, NPT, TB, T])
        rec = sb("rec", [P, 2, TB, H2 // 2])
        yv = sb("yv", [P, TB, D])
        xn_x = yv
        maskrow = sb("maskrow", [P, T])
        keymask = maskrow
        r3 = sb("r3", [P, 4, 16])
        bd = sb("bd", [P, DB, P])
        kmax = sb("kmax", [P, 4, DB])

        class Chain:

            def __init__(self, eng, sem):
                self.eng, self.sem, self.n = eng, sem, 0

            def mark(self, ins):
                self.n += 1
                ins.then_inc(self.sem, 1)
                return self.n

            def done(self, ins):
                self.eng.wait_ge(self.sem, self.mark(ins))

        class Scans:

            def __init__(self, order):
                self.order = order
                self.units = UNITS * len(order)

            def at(self, u):
                return self.order[u // UNITS][0], u % UNITS // N, u % N

            def begins(self, eng, u):
                if u % UNITS == 0 and self.order[u // UNITS][1]:
                    eng.wait_ge(S["prep_done"], self.order[u // UNITS][1])

            def tensor(self, pe, tick):
                for u in range(0, B_AHEAD, 2):
                    self.broadcast_b(pe, u)
                for u in range(self.units + LAG):
                    if u % 2 == 0 and u + B_AHEAD < self.units:
                        self.broadcast_b(pe, u + B_AHEAD)
                    if u >= LAG:
                        self.sum_states(pe, u - LAG)
                    tick(u)

            def broadcast_b(self, pe, u):
                self.begins(pe, u)
                s, _, n = self.at(u)
                if u >= 4:
                    pe.wait_ge(S["dbu_done"], u // 2 - 1)
                for j in range(2):
                    for t in range(TB):
                        last = nc.tensor.matmul(ps_b[:, u // 2 % 2, j * T + t * P:j * T + (t + 1) * P],
                                                bcm[s][:, t, n + j:n + j + 1].broadcast_to([P, P]), ident[:, :],
                                                is_transpose=True, start=True, stop=True)
                last.then_inc(S["b_full"], 1)

            def sum_states(self, pe, u):
                s, hh, n = self.at(u)
                if n == 0:
                    if u >= N:
                        pe.wait_ge(S["y_taken"], u // N)
                    for t in range(TB):
                        for e in range(HALF):
                            last = nc.tensor.matmul(ps_y[:, t, e * P:(e + 1) * P],
                                                    u_s[s][:, hh * HALF + e, t * P:(t + 1) * P], ident[:, :],
                                                    is_transpose=True, start=(t == 0 and e == 0), stop=False,
                                                    skip_group_check=True)
                pe.wait_ge(S["g_ready"], u + 1)
                for t in range(TB):
                    for e in range(HALF):
                        last = nc.tensor.matmul(ps_y[:, t, e * P:(e + 1) * P],
                                                g[:, u % NG, e, t * P:(t + 1) * P], ident[:, :],
                                                is_transpose=True, start=False, stop=(n == N - 1),
                                                skip_group_check=True)
                last.then_inc(S["g_used"], 1)

            def scalar(self, act, tick):
                for u in range(DA_AHEAD):
                    self.decays(act, u)
                for u in range(self.units + LAG):
                    if u + DA_AHEAD < self.units:
                        self.decays(act, u + DA_AHEAD)
                    v = u - LAG
                    if v >= 0 and v % N == N - 1:
                        s, hh, _ = self.at(v)
                        act.wait_ge(S["g_used"], v + 1)
                        nc.scalar.activation(yt[s][:, hh, :, :], ps_y[:, :, :], ACT.Copy).then_inc(S["y_taken"], 1)
                    tick(u)

            def decays(self, act, u):
                self.begins(act, u)
                s, hh, n = self.at(u)
                if u >= DA_AHEAD + 2:
                    act.wait_ge(S["scan_done"], u - DA_AHEAD - 1)
                for e in range(HALF):
                    eb = hh * HALF + e
                    last = nc.scalar.activation(decay[:, u % (DA_AHEAD + 2), e, :], delta[s][:, eb, :], ACT.Exp,
                                                scale=acoef[:, s, eb, n:n + 1])
                last.then_inc(S["da_ready"], 1)

            def with_b(self, dve, u):
                s, hh, _ = self.at(u)
                dve.wait_ge(S["b_full"], u // 2 + 1)
                if u >= 2 * NDBU:
                    dve.wait_ge(S["scan_done"], u - 2 * NDBU + 2)
                nc.vector.tensor_tensor(dbu[:, u // 2 % NDBU, :, :, :],
                                        du[s][:, hh * HALF:(hh + 1) * HALF, :].unsqueeze(1).broadcast_to([P, 2, HALF, T]),
                                        ps_b[:, u // 2 % 2, :].rearrange("p (j t) -> p j t", j=2).unsqueeze(2)
                                        .broadcast_to([P, 2, HALF, T]), ALU.mult).then_inc(S["dbu_done"], 1)

            def vector(self, dve, tick):
                self.with_b(dve, 0)
                for u in range(self.units):
                    if u % 2 == 0:
                        if u + 2 < self.units:
                            self.with_b(dve, u + 2)
                        dve.wait_ge(S["dbu_done"], u // 2 + 1)
                    s, _, _ = self.at(u)
                    dve.wait_ge(S["da_ready"], u + 1)
                    if u >= NHST:
                        dve.wait_ge(S["g_ready"], u - NHST + 1)

                    def line(a):
                        a = a.rearrange("p e t -> p (e t)")
                        return a[:, HALF * T - 1::-1] if s == 1 else a

                    nc.vector.tensor_tensor_scan(line(hst[:, u % NHST, :, :]), line(decay[:, u % (DA_AHEAD + 2), :, :]),
                                                 line(dbu[:, u // 2 % NDBU, u % 2, :, :]), 0.0, ALU.mult,
                                                 ALU.add).then_inc(S["scan_done"], 1)
                    tick(u)
                for u in range(self.units, self.units + LAG):
                    tick(u)

            def gpsimd(self, pool):
                for u in range(self.units):
                    n = u % N
                    if u % UNITS < N and n % CHUNK == 0:
                        pool.wait_ge(S[f"c_in_{n // CHUNK}"], 16 * (u // UNITS + 1))
                    pool.wait_ge(S["scan_done"], u + 1)
                    if u >= NG:
                        pool.wait_ge(S["g_used"], u - NG + 1)
                    nc.gpsimd.tensor_tensor(g[:, u % NG, :, :], hst[:, u % NHST, :, :],
                                            c_bc[:, n, :].unsqueeze(1).broadcast_to([P, HALF, T]),
                                            ALU.mult).then_inc(S["g_ready"], 1)
                pool.wait_ge(S["y_taken"], 2 * len(self.order))
                pool.wait_ge(S["g_used"], self.units)

            def sync(self, sp, tick):
                for j in range(CHUNKS):
                    self.load_c(sp, 0, j)
                for u in range(self.units + LAG):
                    k, v = divmod(u - N - CHUNK, UNITS)
                    if v % CHUNK == 0 and v // CHUNK < CHUNKS and 0 <= k < len(self.order) - 1:
                        if v == 0 and self.order[k + 1][1]:
                            sp.wait_ge(S["c_stored"], 16 * self.order[k + 1][1])
                        sp.wait_ge(S["g_ready"], k * UNITS + N + v + CHUNK)
                        self.load_c(sp, k + 1, v // CHUNK)
                    tick(u)

            def load_c(self, sp, k, j):
                sp.dma_start(c_bc[:, j * CHUNK:(j + 1) * CHUNK, :].rearrange("p n t -> p (n t)"),
                             c_rows[self.order[k][0], j * CHUNK:(j + 1) * CHUNK, :].rearrange("n t -> (n t)")
                             .partition_broadcast(P)).then_inc(S[f"c_in_{j}"], 16)
                self.loads[j] = k + 1

            loads = [0] * CHUNKS

            def wait_c(self, sp):
                for j in range(CHUNKS):
                    if self.loads[j]:
                        sp.wait_ge(S[f"c_in_{j}"], 16 * self.loads[j])

        def norm(ch, slot, src, scale_shift):
            ve = nc.vector
            for t in range(TB):
                last = ch.mark(ve.bn_stats(st[:, slot, t, :], src[:, t, :]))
            ch.eng.wait_ge(ch.sem, last)
            for t in range(TB):
                last = ch.mark(ve.bn_aggr(mv[:, slot, t, :], st[:, slot, t, :]))
            ch.eng.wait_ge(ch.sem, last)
            k = nrm[:, slot, :, :]
            ch.done(ve.tensor_scalar(k[:, 0, :], mv[:, slot, :, 1], EPS, None, ALU.add))
            ch.mark(ve.tensor_scalar(k[:, 1, :], k[:, 0, :], -0.5, None, ALU.mult))
            ch.done(ve.tensor_scalar(k[:, 2, :].bitcast(I32), k[:, 0, :].bitcast(I32), -0.5, 1597463007.0,
                                     ALU.mult, ALU.add))
            a, b = 2, 3
            for _ in range(3):
                ch.done(ve.tensor_tensor(k[:, 4, :], k[:, a, :], k[:, a, :], ALU.mult))
                ch.done(ve.tensor_tensor(k[:, 5, :], k[:, 4, :], k[:, 1, :], ALU.mult))
                ch.done(ve.scalar_tensor_tensor(out=k[:, b, :], in0=k[:, 5, :], scalar=1.5, in1=k[:, a, :],
                                                op0=ALU.add, op1=ALU.mult))
                a, b = b, a
            for t in range(TB):
                last = scale_shift(t, mv[:, slot, t, 0:1], k[:, a, t:t + 1])
            return last

        def plain(src, dst):
            def go(t, mean, inv):
                return nc.vector.tensor_scalar(dst[:, t, :], src[:, t, :], mean, inv, ALU.subtract, ALU.mult)
            return go

        def turn(src, dst, full):
            for d in range(DB):
                for t in range(TB):
                    last = nc.tensor.matmul(dst[:, d, t * P:(t + 1) * P], src[:, t, d * P:(d + 1) * P],
                                            ident[:, :], is_transpose=True, start=True, stop=True)
            last.then_inc(full, 1)

        def project(dst, weight, m0, m, rhs, kb):
            for k in range(kb):
                last = nc.tensor.matmul(dst, weight[:, k, m0:m0 + m], rhs[:, k, :], start=(k == 0), stop=(k == kb - 1))
            return last

        def to_tokens(dst, lhs, t, weight, kb, bias=None):
            for k in range(kb):
                last = nc.tensor.matmul(dst, lhs[:, k, t * P:(t + 1) * P], weight[:, k, :], start=(k == 0),
                                        stop=(bias is None and k == kb - 1))
            if bias is not None:
                last = nc.tensor.matmul(dst, ones[R:R + 1, :], brow[0:1, BIASROWS.index(bias), :], start=False, stop=True)
            return last

        def prep_tensor(pe, s, r, t0):
            project(ps_v[0:R, P:P + T], (w["wdlt0"], w["wdlt1"], w["wdlt2"])[s], 0, R, u_s[s], EB).then_inc(S["dlt_full"], 1)
            pe.wait_ge(S["dlt_full"], r + 1)
            for t in range(TB):
                last = to_tokens(ps_v[:, t * 2 * N:(t + 1) * 2 * N], u_s[s], t, (w["wbc0"], w["wbc1"], w["wbc2"])[s], EB)
            last.then_inc(S["bc_full"], 1)
            yield t0 + 1
            pe.wait_ge(S["bc_sb"], r + 1)
            for t in range(TB):
                last = nc.tensor.matmul(ps_v[0:N, t * P:(t + 1) * P], bcm[s][:, t, N:2 * N], ident[:, :],
                                        is_transpose=True, start=True, stop=True)
            last.then_inc(S["ct_full"], 1)
            yield t0 + 2
            pe.wait_ge(S["ct_sb"], r + 1)
            for k in range(2):
                if k == 1:
                    pe.wait_ge(S["dt_read"], 2 * r + 1)
                for j in range(2):
                    eb = 2 * k + j
                    last = nc.tensor.matmul(pair[:, j, :], wdt[:, s, eb * P:(eb + 1) * P], dlt, start=True, stop=True)
                last.then_inc(S["dt_full"], 1)
                yield t0 + 3 + k
            pe.wait_ge(S["dt_read"], 2 * r + 2)

        def prep_scalar(act, s, r, t0):
            act.wait_ge(S["bc_full"], r + 1)
            if r >= 1:
                act.wait_ge(S["dt_full"], 2 * r)
            nc.scalar.activation(dlt, ps_v[0:R, P:P + T], ACT.Copy)
            nc.scalar.activation(bcm[s][:, :, :].rearrange("p t n -> p (t n)"), ps_v[:, 0:TB * 2 * N],
                                 ACT.Copy).then_inc(S["bc_sb"], 1)
            yield t0 + 1
            act.wait_ge(S["ct_full"], r + 1)
            if r >= 1:
                act.wait_ge(S["c_stored"], 16 * r)
            nc.scalar.activation(ct, ps_v[0:N, 0:T], ACT.Copy).then_inc(S["ct_sb"], 1)
            yield t0 + 4
            act.wait_ge(S["sp_clip"], 2 * r + 2)
            ch = act_chain[0]
            ch.done(nc.scalar.activation(soft, soft, ACT.Exp))
            nc.scalar.activation(soft, soft, ACT.Ln, bias=1.0).then_inc(S["sp_log"], 1)
            if s == 1:
                nc.scalar.activation(act_x[:, :, :], act_x[:, :, :], ACT.Silu)

        def prep_vector(dve, ch, s, r, edge, t0):
            bdt = (c["bdt0"], c["bdt1"], c["bdt2"])[s]
            for k in range(2):
                dve.wait_ge(S["dt_full"], 2 * r + k + 1)
                for j in range(2):
                    eb = 2 * k + j
                    last = nc.vector.tensor_scalar(soft[:, eb, :], pair[:, j, :], bdt[:, eb:eb + 1], 30.0,
                                                   ALU.add, ALU.min)
                last.then_inc(S["sp_clip"], 1)
                for j in range(2):
                    eb = 2 * k + j
                    last = nc.vector.tensor_scalar(delta[s][:, eb, :], pair[:, j, :], bdt[:, eb:eb + 1], None, ALU.add)
                last.then_inc(S["dt_read"], 1)
                yield t0 + 3 + 2 * k
            dve.wait_ge(S["dt_read"], 2 * r + 2)
            dve.wait_ge(S["sp_log"], r + 1)
            ch.done(nc.vector.tensor_tensor(delta[s][:, :, :], delta[s][:, :, :], soft, ALU.max))
            ch.done(nc.vector.tensor_tensor(du[s][:, :, :], delta[s][:, :, :], u_s[s][:, :, :], ALU.mult))
            yield t0 + 6
            for eb in range(EB):
                last = ch.mark(nc.vector.tensor_scalar(u_s[s][:, eb, :], u_s[s][:, eb, :],
                                                       (c["dp0"], c["dp1"], c["dp2"])[s][:, eb:eb + 1], None, ALU.mult))
            ch.done(nc.vector.memset(delta[s][:, :, edge:edge + 1], RESET))
            nc.vector.engine_nop().then_inc(S["prep_done"], 1)

        def prep_sync(sp, scans, s, r):
            sp.wait_ge(S["ct_sb"], r + 1)
            if scans:
                scans.wait_c(sp)
            sp.dma_start(c_rows[s], ct).then_inc(S["c_stored"], 16)
            sp.wait_ge(S["c_stored"], 16 * (r + 1))

        def l0_pre_sync(sp, b):
            sp.dma_start(x0[:, :, :], dram["x"][bass.ds(b, 1)].rearrange("b (k p) d -> p (b k) d", p=P)).then_inc(S["x_in"], 16)
            sp.dma_start(rows_bc[:, :, :].rearrange("p r d -> p (r d)"),
                         mod_rows[bass.ds(b, 1), 0:3 * D].rearrange("b d -> (b d)").partition_broadcast(P)).then_inc(S["row_in"], 16)

        def l0_pre_vector(dve, ch, r, t0):
            dve.wait_ge(S["x_in"], 16)
            dve.wait_ge(S["row_in"], 16)

            def modulate(t, mean, inv):
                ch.done(nc.vector.scalar_tensor_tensor(out=tmp[:, t, :], in0=x0[:, t, :], scalar=mean,
                                                       in1=rows_bc[:, 0, :], op0=ALU.subtract, op1=ALU.mult))
                return nc.vector.scalar_tensor_tensor(out=xa[:, t, :], in0=tmp[:, t, :], scalar=inv,
                                                      in1=rows_bc[:, 1, :], op0=ALU.mult, op1=ALU.add)

            ch.done(norm(ch, 0, x0, modulate))
            yield t0 + 3
            norm(ch, 1, xa, plain(xa, xn)).then_inc(S["xn_a"], 1)
            yield t0 + 6
            dve.wait_ge(S["xn_a"], 1)
            ch.done(nc.vector.tensor_tensor(xa[:, :, :], xa[:, :, :], rows_bc[:, 2, :].unsqueeze(1).broadcast_to([P, TB, D]),
                                            ALU.mult))
            ch.done(nc.vector.tensor_tensor(x0[:, :, :], x0[:, :, :], xa[:, :, :], ALU.add))
            yield t0 + 9
            yield from prep_vector(dve, ch, 0, r, 0, t0 + 7)

        def l0_pre_tensor(pe, r, t0):
            pe.wait_ge(S["xn_a"], 1)
            turn(xn, pair, S["xt_full_a"])
            yield t0 + 5
            pe.wait_ge(S["xt_sb_a"], 1)
            for k in range(2):
                if k == 1:
                    pe.wait_ge(S["z_sb"], 1)
                for j in range(2):
                    last = project(pair[:, j, :], z1w, (2 * k + j) * P, P, xT, DB)
                last.then_inc(S["z_full"], 1)
                yield t0 + 6 + k
            pe.wait_ge(S["z_sb"], 2)
            yield from prep_tensor(pe, 0, r, t0 + 7)
            for k in range(4):
                if k >= 1:
                    pe.wait_ge((S["mx_sb"], S["mx_sb"], S["z_sb"])[k - 1], (1, 2, 3)[k - 1])
                for j in range(2):
                    last = project(pair[:, j, :], (w["wx"], z2w)[k // 2], (2 * (k % 2) + j) * P, P, xT, DB)
                last.then_inc((S["mx_full"], S["z_full"])[k // 2], 1)
                yield t0 + 12 + k
            pe.wait_ge(S["z_sb"], 4)

        def l0_pre_scalar(act, r, t0):
            act.wait_ge(S["xt_full_a"], 1)
            for d in range(DB):
                last = nc.scalar.activation(xT[:, d, :], pair[:, d, :], ACT.Identity, scale=c["n2g"][:, d:d + 1],
                                            bias=c["n2b"][:, d:d + 1])
            last.then_inc(S["xt_sb_a"], 1)
            yield t0 + 5
            for k in range(2):
                take_z(act, k)
                yield t0 + 6 + k
            yield from prep_scalar(act, 0, r, t0 + 7)
            for k in range(2):
                act.wait_ge(S["mx_full"], k + 1)
                for j in range(2):
                    eb = 2 * k + j
                    last = nc.scalar.activation(act_x[:, eb, :], pair[:, j, :], ACT.Identity, bias=c["bx"][:, eb:eb + 1])
                last.then_inc(S["mx_sb"], 1)
                yield t0 + 12 + k
            for k in range(2, 4):
                take_z(act, k)
                yield t0 + 12 + k

        def take_z(act, k):
            act.wait_ge(S["z_full"], k + 1)
            for j in range(2):
                eb = 2 * (k % 2) + j
                last = nc.scalar.activation(u_s[k // 2][:, eb, :], pair[:, j, :], ACT.Identity,
                                            bias=(z1b, z2b)[k // 2][:, eb:eb + 1])
            last.then_inc(S["z_sb"], 1)

        def l0_post_tensor(pe, t0):
            pe.wait_ge(S["y_taken"], 4)
            for k in range(2):
                if k == 1:
                    pe.wait_ge(S["yg_0"], 1)
                for j in range(2):
                    for t in range(TB):
                        for s in range(2):
                            last = nc.tensor.matmul(pair[:, j, t * P:(t + 1) * P],
                                                    yt[s][:, k, t, j * P:(j + 1) * P], ident[:, :], is_transpose=True,
                                                    start=(j == 0 and t == 0 and s == 0), stop=(s == 1),
                                                    skip_group_check=True)
                last.then_inc(S["yb_full_0"], 1)
                yield t0 + 1 + k
            pe.wait_ge(S["yg_0"], 2)
            for t in range(TB):
                last = to_tokens(pair[:, t, :], yg, t, w["wf"], EB, "bf")
                if t == 0:
                    yield t0 + 3
            last.then_inc(S["o_full_0"], 1)
            yield t0 + 4
            pe.wait_ge(S["res_0"], 1)

        def l0_post_vector(dve, ch, t0):
            for k in range(2):
                dve.wait_ge(S["yb_full_0"], k + 1)
                nc.vector.tensor_tensor(yg[:, 2 * k:2 * k + 2, :], pair, act_x[:, 2 * k:2 * k + 2, :],
                                        ALU.mult).then_inc(S["yg_0"], 1)
                yield t0 + 1 + 2 * k
            dve.wait_ge(S["o_full_0"], 1)
            ch.done(nc.vector.tensor_tensor(x1[:, :, :], pair, rows_bc[:, 2, :].unsqueeze(1).broadcast_to([P, TB, D]),
                                            ALU.mult))
            ins = nc.vector.tensor_tensor(x1[:, :, :], x1[:, :, :], x0[:, :, :], ALU.add)
            ins.then_inc(S["res_0"], 1)
            dve.wait_ge(S["res_0"], 1)

        def l1_pre_vector(dve, ch, b, r, t0):
            if r >= 1:
                dve.wait_ge(S["c_stored"], 16 * r)
            ch.done(nc.vector.tensor_copy(xr[:, :, :], x1[:, :, :]))
            nc.vector.tensor_copy(cols1[:, :].unsqueeze(2), mod_cols[:, 0:2 * DB, bass.ds(b, 1)]).then_inc(S["cols_now"], 1)
            norm(ch, 2, x1, plain(x1, xn)).then_inc(S["xn_b"], 1)
            yield t0 + 2
            nc.vector.memset(xm[:, :, 0:CT - 1], 0.0)
            for k in range(2):
                dve.wait_ge(S["xm_full"], k + 1)
                ch.mark(nc.vector.tensor_copy(xm[:, 2 * k:2 * k + 2, CT - 1:CT - 1 + T], pair))
                for j in range(2):
                    eb = 2 * k + j
                    last = nc.vector.tensor_scalar(acc[:, eb, :], pair[:, j, :],
                                                   c["convw"][:, eb * CT + CT - 1:eb * CT + CT], c["convb"][:, eb:eb + 1],
                                                   ALU.mult, ALU.add)
                last.then_inc(S["xm_sb"], 1)
                yield t0 + 3 + k
            dve.wait_ge(S["xm_sb"], 2)
            for tap in range(CT - 1):
                for eb in range(EB):
                    last = nc.vector.scalar_tensor_tensor(
                        out=acc[:, eb, :], in0=xm[:, eb, tap:tap + T], scalar=c["convw"][:, eb * CT + tap:eb * CT + tap + 1],
                        in1=acc[:, eb, :], op0=ALU.mult, op1=ALU.add)
                    last.then_inc(S["conv_done"], 1)
                dve.wait_ge(S["conv_done"], (tap + 1) * EB)
                yield t0 + 5 + tap
            yield t0 + 10
            yield from prep_vector(dve, ch, 2, r, 0, t0 + 8)

        def l1_pre_tensor(pe, r, t0):
            pe.wait_ge(S["xn_b"], 1)
            for d in range(DB):
                for t in range(TB):
                    last = nc.tensor.matmul(pair[:, d, :], xn[:, t, d * P:(d + 1) * P], gath[:, t, :],
                                            start=(t == 0), stop=(t == TB - 1))
            last.then_inc(S["xt_full_b"], 1)
            yield t0 + 2
            pe.wait_ge(S["xt_sb_b"], 1)
            for k in range(2):
                if k == 1:
                    pe.wait_ge(S["xm_sb"], 1)
                for j in range(2):
                    last = project(pair[:, j, :], w["win"], (2 * k + j) * P, P, xT, DB)
                last.then_inc(S["xm_full"], 1)
                yield t0 + 3 + k
            for k in range(2):
                if k == 0:
                    pe.wait_ge(S["xm_sb"], 2)
                if k == 1:
                    pe.wait_ge(S["gz_sb"], 1)
                for j in range(2):
                    last = project(pair[:, j, :], w["win"], E + (2 * k + j) * P, P, xT, DB)
                last.then_inc(S["gz_full"], 1)
                yield t0 + 5 + k
            yield t0 + 8
            pe.wait_ge(S["gz_sb"], 2)
            pe.wait_ge(S["conv_silu"], 1)
            yield from prep_tensor(pe, 2, r, t0 + 8)

        def l1_pre_scalar(act, r, t0):
            act.wait_ge(S["cols_now"], 1)
            act.wait_ge(S["xt_full_b"], 1)
            for d in range(DB):
                last = nc.scalar.activation(xT[:, d, :], pair[:, d, :], ACT.Identity, scale=cols1[:, d:d + 1],
                                            bias=cols1[:, DB + d:DB + d + 1])
            last.then_inc(S["xt_sb_b"], 1)
            yield t0 + 4
            for k in range(2):
                act.wait_ge(S["gz_full"], k + 1)
                nc.scalar.activation(act_z[:, 2 * k:2 * k + 2, :], pair, ACT.Copy).then_inc(S["gz_sb"], 1)
                yield t0 + (5, 7)[k]
            act.wait_ge(S["conv_done"], (CT - 1) * EB)
            act.wait_ge(S["gz_sb"], 2)
            nc.scalar.activation(act_z[:, :, :], act_z[:, :, :], ACT.Silu)
            nc.scalar.activation(u_s[2][:, :, :], acc[:, :, :], ACT.Silu).then_inc(S["conv_silu"], 1)
            yield t0 + 8
            yield from prep_scalar(act, 2, r, t0 + 8)

        def l1_post_tensor(pe, t0):
            for k in range(2):
                if k == 1:
                    pe.wait_ge(S["yg_1"], 1)
                for j in range(2):
                    for t in range(TB):
                        last = nc.tensor.matmul(pair[:, j, t * P:(t + 1) * P], yt[2][:, k, t, j * P:(j + 1) * P],
                                                ident[:, :], is_transpose=True, start=True, stop=True)
                last.then_inc(S["yb_full_1"], 1)
                yield t0 + 1 + k
            pe.wait_ge(S["yg_1"], 2)
            for t in range(TB):
                last = to_tokens(pair[:, t, :], yg, t, w["wout1"], EB)
                if t == 0:
                    yield t0 + 3
            last.then_inc(S["o_full_1"], 1)
            yield t0 + 4
            pe.wait_ge(S["o_sb_1"], 1)
            for q in range(TB):
                for t in range(TB):
                    last = nc.tensor.matmul(pair[:, q, :], gath[:, t, q * P:(q + 1) * P], tmp[:, t, :],
                                            start=(t == 0), stop=(t == TB - 1))
            last.then_inc(S["og_full_1"], 1)
            yield t0 + 5
            pe.wait_ge(S["res_1"], 1)

        def l1_post_scalar(act, t0):
            act.wait_ge(S["o_full_1"], 1)
            nc.scalar.activation(tmp[:, :, :], pair, ACT.Copy).then_inc(S["o_sb_1"], 1)
            yield t0 + 4

        def l1_post_vector(dve, ch, t0):
            for k in range(2):
                dve.wait_ge(S["yb_full_1"], k + 1)
                nc.vector.tensor_tensor(yg[:, 2 * k:2 * k + 2, :], pair, act_z[:, 2 * k:2 * k + 2, :],
                                        ALU.mult).then_inc(S["yg_1"], 1)
                yield t0 + 1 + 3 * k
            dve.wait_ge(S["gate_in"], 16)
            dve.wait_ge(S["og_full_1"], 1)
            ch.done(nc.vector.tensor_tensor(x2[:, :, :], pair, gate1[:, :].unsqueeze(1).broadcast_to([P, TB, D]),
                                            ALU.mult))
            nc.vector.tensor_tensor(x2[:, :, :], x2[:, :, :], xr[:, :, :], ALU.add).then_inc(S["res_1"], 1)
            dve.wait_ge(S["res_1"], 1)

        def l1_post_sync(sp, b):
            sp.dma_start(gate1[:, :], mod_rows[bass.ds(b, 1), 3 * D:4 * D].rearrange("b d -> (b d)")
                         .partition_broadcast(P)).then_inc(S["gate_in"], 16)

        def tail_tensor(pe, weight, bias, yn, yt_full, yt_sb, h_full, res, t0):
            pe.wait_ge(yn, 1)
            turn(xn_x, bank(0, DB), yt_full)
            yield t0 + 3
            pe.wait_ge(yt_sb, 1)
            for t in range(TB):
                last = to_tokens(bank(1, TB)[:, t, :], xT_x, t, weight, DB, bias)
            last.then_inc(h_full, 1)
            yield t0 + 5
            pe.wait_ge(res, 1)
            yield t0 + 5

        def tail_scalar(act, k, yt_full, yt_sb, t0):
            act.wait_ge(yt_full, 1)
            for d in range(DB):
                last = nc.scalar.activation(xT_x[:, d, :], bank(0, DB)[:, d, :], ACT.Silu,
                                            scale=cols23[:, k * DB + d:k * DB + d + 1],
                                            bias=cols23[:, (k + 1) * DB + d:(k + 1) * DB + d + 1])
            last.then_inc(yt_sb, 1)
            yield t0 + 3

        def tail_vector(dve, ch, slot, yn, h_full, res, t0):
            norm(ch, slot, yv, plain(yv, xn_x)).then_inc(yn, 1)
            yield t0 + 4
            dve.wait_ge(h_full, 1)
            nc.vector.tensor_tensor(x2[:, :, :], bank(1, TB), x2[:, :, :], ALU.add).then_inc(res, 1)
            dve.wait_ge(res, 1)
            yield t0 + 5

        def l2_tensor(pe, t0):
            pe.wait_ge(S["xn_c"], 1)
            turn(xn_x, bank(0, DB), S["xt_full_c"])
            yield t0 + 3
            pe.wait_ge(S["xt_sb_c"], 1)
            for k in range(4):
                if k == 3:
                    pe.wait_ge(S["q_sb"], 1)
                for j in range(2):
                    last = project(bank((1, 2, 3, 1)[k], 2)[:, j, :], (w["wq2"], w["wk2"])[k // 2], (2 * (k % 2) + j) * P, P, xT_x, DB)
                last.then_inc(S["qk_full"], 1)
                yield t0 + 4 + k
            for t in range(TB):
                last = to_tokens(bank(0, TB)[:, t, :], xT_x, t, w["wv2"], DB, "bv2")
            last.then_inc(S["v2_full"], 1)
            yield t0 + 9
            pe.wait_ge(S["v2_sb"], 1)
            pe.wait_ge(S["q_sb"], 2)
            pe.wait_ge(S["k_sb"], 4)
            for h in range(H2 + PV_LAG):
                if h < H2:
                    if h >= 2:
                        pe.wait_ge(S["s_max"], h - 1)
                    r, hb = 32 * (h % HPB), h // HPB
                    for q in range(TB):
                        last = nc.tensor.matmul(bank(S_BANKS[h % 2], TB)[:, q, :], qT[r:r + DH2 + 1, hb, q * P:(q + 1) * P],
                                                kT[r:r + DH2 + 1, hb, :], start=True, stop=True)
                    last.then_inc(S["s_full"], 1)
                if 2 <= h < H2 + 2:
                    v = h - 2
                    pe.wait_ge(S["p_ready"], v + 1)
                    if v >= 1:
                        pe.wait_ge(S["pt_sb"], v)
                    for m in range(TB):
                        for q in range(TB):
                            last = nc.tensor.matmul(bank(1, TB)[:, m, q * P:(q + 1) * P],
                                                    pr[:, v % NSC, q, m * P:(m + 1) * P], ident[:, :],
                                                    is_transpose=True, start=True, stop=True)
                    last.then_inc(S["pt_full"], 1)
                if h >= PV_LAG:
                    v = h - PV_LAG
                    pe.wait_ge(S["pt_sb"], v + 1)
                    if v == H2 // 2:
                        pe.wait_ge(S["o_taken_2"], 1)
                    o = bank(2, TB).rearrange("p q (h l) -> p q h l", l=32)[:, :, v % 8, 0:DH2 + 1]
                    for q in range(TB):
                        for m in range(TB):
                            last = nc.tensor.matmul(o[:, q, :], pT[:, v % NPT, m, q * P:(q + 1) * P], v2[:, m, v, :],
                                                    start=(m == 0 and q == 0 and v % 8 == 0), stop=(m == TB - 1),
                                                    skip_group_check=True)
                    last.then_inc(S["o_full_2"], 1)
                yield t0 + 10 + h
            pe.wait_ge(S["o_taken_2"], 2)
            yield from tail_tensor(pe, w["wo2"], "bo2", S["yn_2"], S["yt_full_2"], S["yt_sb_2"], S["h_full_2"], S["res_2"], t0 + 28)

        def l2_scalar(act, t0):
            act.wait_ge(S["xt_full_c"], 1)
            for d in range(DB):
                last = nc.scalar.activation(xT_x[:, d, :], bank(0, DB)[:, d, :], ACT.Identity, scale=c["l2w"][:, d:d + 1],
                                            bias=c["l2b"][:, d:d + 1])
            last.then_inc(S["xt_sb_c"], 1)
            yield t0 + 4
            for k in range(2):
                act.wait_ge(S["qk_full"], k + 1)
                for j in range(2):
                    hb = 2 * k + j
                    last = nc.scalar.activation(qT[:, hb, :], bank(1 + k, 2)[:, j, :], ACT.Identity,
                                                bias=c["bq2"][:, hb:hb + 1])
                last.then_inc(S["q_sb"], 1)
                yield t0 + 5 + k
            yield t0 + 8
            act.wait_ge(S["v2_full"], 1)
            for t in range(TB):
                last = nc.scalar.activation(v2[:, t, :, 0:DH2], bank(0, TB)[:, t, :].rearrange("p (h l) -> p h l", l=DH2),
                                            ACT.Copy, scale=masks[:, t:t + 1])
            last.then_inc(S["v2_sb"], 1)
            yield t0 + 10
            for h in range(H2):
                act.wait_ge(S["s_max"], h + 1)
                for q in range(TB):
                    last = nc.scalar.activation(pr[:, h % NSC, q, :], pr[:, h % NSC, q, :], ACT.Exp,
                                                bias=mx[:, h % 2, 1, q:q + 1])
                last.then_inc(S["p_ready"], 1)
                if h >= 1:
                    self_copy(act, h - 1)
                yield t0 + 11 + h
            self_copy(act, H2 - 1)
            yield t0 + 30
            yield from tail_scalar(act, 0, S["yt_full_2"], S["yt_sb_2"], t0 + 28)

        def self_copy(act, v):
            act.wait_ge(S["pt_full"], v + 1)
            if v >= NPT:
                act.wait_ge(S["o_full_2"], v - NPT + 1)
            nc.scalar.activation(pT[:, v % NPT, :, :], bank(1, TB), ACT.Copy).then_inc(S["pt_sb"], 1)

        def l2_vector(dve, ch, b, t0):
            ch.done(nc.vector.tensor_copy(cols23[:, :].unsqueeze(2), mod_cols[:, 2 * DB:6 * DB, bass.ds(b, 1)]))
            ch.done(nc.vector.tensor_copy(masks[:, 0:TB], c["mask2"][:, bass.ds(b * TB, TB)]))
            ch.done(nc.vector.tensor_copy(masks[:, TB:2 * TB], c["mask3"][:, bass.ds(b * TB, TB)]))
            ch.done(nc.vector.memset(v2[:, :, :, DH2:DH2 + 1], 1.0))
            norm(ch, 3, x2, plain(x2, xn_x)).then_inc(S["xn_c"], 1)
            yield t0 + 6
            dve.wait_ge(S["key_in"], 16)
            ch.done(nc.vector.tensor_scalar(keymask[:, :], keymask[:, :], 1.0, c["keyrow"][:, 0:1], ALU.subtract, ALU.mult))
            for k in range(2):
                dve.wait_ge(S["qk_full"], 3 + k)
                for j in range(2):
                    hb = 2 * k + j
                    nc.vector.scalar_tensor_tensor(out=kT[:, hb, :], in0=bank((3, 1)[k], 2)[:, j, :],
                                                   scalar=c["bk2"][:, hb:hb + 1], in1=keymask[:, :], op0=ALU.add,
                                                   op1=ALU.add).then_inc(S["k_sb"], 1)
                yield t0 + 7 + k
            yield t0 + 9
            for h in range(H2):
                dve.wait_ge(S["s_full"], h + 1)
                if h >= NSC:
                    dve.wait_ge(S["pt_full"], h - NSC + 1)
                if h >= 2:
                    dve.wait_ge(S["p_ready"], h - 1)
                for q in range(TB):
                    last = ch.mark(nc.vector.tensor_scalar(pr[:, h % NSC, q, :], bank(S_BANKS[h % 2], TB)[:, q, :],
                                                           0.0, None, ALU.add, ALU.max,
                                                           accum_out=mx[:, h % 2, 0, q:q + 1]))
                dve.wait_ge(S["dve_chain"], last)
                nc.vector.tensor_scalar(mx[:, h % 2, 1, :], mx[:, h % 2, 0, :], -1.0, None, ALU.mult).then_inc(S["s_max"], 1)
                if h == H2 // 2 + PV_LAG - 1:
                    take_heads(dve, ch, 0)
                yield t0 + 10 + h
            yield t0 + 28
            take_heads(dve, ch, 1)
            yield from tail_vector(dve, ch, 0, S["yn_2"], S["h_full_2"], S["res_2"], t0 + 28)

        def take_heads(dve, ch, half):
            dve.wait_ge(S["o_full_2"], (half + 1) * H2 // 2)
            o = bank(2, TB).rearrange("p q (h l) -> p q h l", l=32)
            for q in range(TB):
                last = ch.mark(nc.vector.reciprocal(rec[:, half, q, :].unsqueeze(2), o[:, q, :, DH2:DH2 + 1]))
            dve.wait_ge(S["dve_chain"], last)
            for q in range(TB):
                last = ch.mark(nc.vector.tensor_tensor(
                    yv[:, q, half * P:(half + 1) * P].rearrange("p (h l) -> p h l", l=DH2), o[:, q, :, 0:DH2],
                    rec[:, half, q, :].unsqueeze(2).broadcast_to([P, H2 // 2, DH2]), ALU.mult))
            dve.wait_ge(S["dve_chain"], last)
            nc.vector.engine_nop().then_inc(S["o_taken_2"], 1)

        def l3_tensor(pe, t0):
            pe.wait_ge(S["xn_d"], 1)
            turn(xn_x, bank(0, DB), S["xt_full_d"])
            yield t0 + 3
            pe.wait_ge(S["xt_sb_d"], 1)
            for t in range(TB):
                last = to_tokens(bank(1, TB)[:, t, :], xT_x, t, w["wq3"], DB, "bq3")
            last.then_inc(S["qkv_full"], 1)
            yield t0 + 4
            for d in range(DB):
                last = project(bank(2, DB)[:, d, :], w["wk3"], d * P, P, xT_x, DB)
            last.then_inc(S["qkv_full"], 1)
            yield t0 + 5
            for t in range(TB):
                last = to_tokens(bank(0, TB)[:, t, :], xT_x, t, w["wv3"], DB, "bv3")
            last.then_inc(S["qkv_full"], 1)
            yield t0 + 7
            pe.wait_ge(S["q_exp"], 1)
            turn(pr[:, 0, :, :], bank(1, DB), S["qk3_t"])
            pe.wait_ge(S["k_exp"], DB)
            for t in range(TB):
                for d in range(DB):
                    last = nc.tensor.matmul(bank(2, TB)[:, t, d * P:(d + 1) * P], pr[:, 1, d, t * P:(t + 1) * P],
                                            ident[:, :], is_transpose=True, start=True, stop=True)
            last.then_inc(S["qk3_t"], 1)
            yield t0 + 9
            pe.wait_ge(S["qk3_sb"], 2)
            pe.wait_ge(S["v3_sb"], 1)
            for d in range(DB):
                for t in range(TB):
                    last = nc.tensor.matmul(bank(0)[:, d * P:(d + 1) * P], pT[:, 1, t, d * P:(d + 1) * P],
                                            v3[:, t, d * P:(d + 1) * P], start=(t == 0), stop=(t == TB - 1))
            last.then_inc(S["bd_full"], 1)
            yield t0 + 11
            pe.wait_ge(S["bd_sb"], DB)
            for t in range(TB):
                for d in range(DB):
                    last = nc.tensor.matmul(bank(1, TB)[:, t, d * P:(d + 1) * P], pT[:, 0, d, t * P:(t + 1) * P],
                                            bd[:, d, :], start=True, stop=True)
            last.then_inc(S["y3_full"], 1)
            yield t0 + 13
            yield from tail_tensor(pe, w["wo3"], "bo3", S["yn_3"], S["yt_full_3"], S["yt_sb_3"], S["h_full_3"], S["res_3"], t0 + 12)

        def l3_scalar(act, t0):
            act.wait_ge(S["xt_full_d"], 1)
            for d in range(DB):
                last = nc.scalar.activation(xT_x[:, d, :], bank(0, DB)[:, d, :], ACT.Identity, scale=c["l3w"][:, d:d + 1],
                                            bias=c["l3b"][:, d:d + 1])
            last.then_inc(S["xt_sb_d"], 1)
            yield t0 + 6
            act.wait_ge(S["qkv_full"], 3)
            for t in range(TB):
                last = nc.scalar.activation(v3[:, t, :], bank(0, TB)[:, t, :], ACT.Copy, scale=masks[:, TB + t:TB + t + 1])
            last.then_inc(S["v3_sb"], 1)
            act.wait_ge(S["q_sub"], 1)
            nc.scalar.activation(pr[:, 0, :, :], pr[:, 0, :, :], ACT.Exp).then_inc(S["q_exp"], 1)
            act.wait_ge(S["k_sub"], 1)
            for d in range(DB):
                nc.scalar.activation(pr[:, 1, d, :], pr[:, 1, d, :], ACT.Exp, bias=kmax[:, 1, d:d + 1],
                                     accum_out=kmax[:, 2, d:d + 1]).then_inc(S["k_exp"], 1)
            yield t0 + 8
            for k in range(2):
                act.wait_ge(S["qk3_t"], k + 1)
                nc.scalar.activation(pT[:, k, :, :], bank(1 + k, 2), ACT.Copy).then_inc(S["qk3_sb"], 1)
            yield t0 + 14
            yield from tail_scalar(act, 2, S["yt_full_3"], S["yt_sb_3"], t0 + 12)

        def l3_vector(dve, ch, t0):
            dve.wait_ge(S["mask_in"], 16)
            ch.done(nc.vector.tensor_scalar(maskrow[:, :], maskrow[:, :], 1.0, NEG, ALU.subtract, ALU.mult))
            norm(ch, 1, x2, plain(x2, xn_x)).then_inc(S["xn_d"], 1)
            yield t0 + 4
            dve.wait_ge(S["qkv_full"], 1)
            q = bank(1).rearrange("p (g l) -> p g l", l=DH3)
            ch.done(nc.vector.tensor_reduce(r3[:, 0, :], q, AX.X, ALU.max))
            nc.vector.tensor_tensor(pr[:, 0, :, :].rearrange("p t (h l) -> p (t h) l", l=DH3), q,
                                    r3[:, 0, :].unsqueeze(2).broadcast_to([P, TB * H3, DH3]),
                                    ALU.subtract).then_inc(S["q_sub"], 1)
            yield t0 + 5
            dve.wait_ge(S["qkv_full"], 2)
            for d in range(DB):
                last = ch.mark(nc.vector.scalar_tensor_tensor(
                    out=pr[:, 1, d, :], in0=bank(2, DB)[:, d, :], scalar=c["bk3"][:, d:d + 1], in1=maskrow[:, :],
                    op0=ALU.add, op1=ALU.add))
            dve.wait_ge(S["dve_chain"], last)
            ch.done(nc.vector.tensor_reduce(kmax[:, 0, :], pr[:, 1, :, :], AX.X, ALU.max))
            nc.vector.tensor_scalar(kmax[:, 1, :], kmax[:, 0, :], -1.0, None, ALU.mult).then_inc(S["k_sub"], 1)
            yield t0 + 7
            dve.wait_ge(S["q_exp"], 1)
            ch.done(nc.vector.tensor_reduce(r3[:, 1, :], pr[:, 0, :, :].rearrange("p t (h l) -> p (t h) l", l=DH3),
                                            AX.X, ALU.add))
            ch.mark(nc.vector.reciprocal(r3[:, 2, :], r3[:, 1, :]))
            dve.wait_ge(S["k_exp"], DB)
            ch.done(nc.vector.reciprocal(kmax[:, 3, :], kmax[:, 2, :]))
            yield t0 + 10
            dve.wait_ge(S["bd_full"], 1)
            for d in range(DB):
                nc.vector.scalar_tensor_tensor(out=bd[:, d, :], in0=bank(0)[:, d * P:(d + 1) * P],
                                               scalar=kmax[:, 3, d:d + 1], in1=blockmask[:, :], op0=ALU.mult,
                                               op1=ALU.mult).then_inc(S["bd_sb"], 1)
            yield t0 + 12
            dve.wait_ge(S["y3_full"], 1)
            ch.done(nc.vector.tensor_tensor(yv[:, :, :].rearrange("p t (h l) -> p (t h) l", l=DH3),
                                            bank(1).rearrange("p (g l) -> p g l", l=DH3),
                                            r3[:, 2, :].unsqueeze(2).broadcast_to([P, TB * H3, DH3]), ALU.mult))
            yield t0 + 12
            yield from tail_vector(dve, ch, 2, S["yn_3"], S["h_full_3"], S["res_3"], t0 + 12)

        def l2_sync(sp, b):
            sp.dma_start(keymask[:, :], dram["mask2"][bass.ds(b, 1), :].rearrange("b d -> (b d)")
                         .partition_broadcast(P)).then_inc(S["key_in"], 16)

        def l3_sync(sp, b):
            sp.dma_start(maskrow[:, :], dram["mask3"][bass.ds(b, 1), :].rearrange("b d -> (b d)")
                         .partition_broadcast(P)).then_inc(S["mask_in"], 16)

        v3 = v2[:, :, :, :].rearrange("p t h l -> p (t h l)")[:, 0:TB * D].rearrange("p (t d) -> p t d", t=TB)
        act_chain = [None]

        STAGES = dict(l0_post=(4, 0, 0, 0, 0), l0_pre=(16, 4, 4, 1, 0), prep1=(7, 0, 0, 2, 1),
                      l1_post=(6, 0, 3, 0, 0), l1_pre=(15, 1, 1, 0, 0),
                      l2=(33, 1, 2, 0, 0), l3=(17, 1, 2, 0, 0))
        TENSOR, SCALAR, VECTOR, SYNC = 1, 2, 3, 4

        def run(order, *groups):
            scans = Scans(order) if order else None
            names = [name for _, _, stages in groups for name, _ in stages]
            preps = [n for n in names if n in ("prep1", "l1_pre", "l0_pre")]
            count = {n: r for r, n in enumerate(preps)}

            def pieces(stages, table, engine):
                t0 = 0
                for name, b in stages:
                    if name in table:
                        yield t0 + STAGES[name][engine]
                        yield from table[name](b, t0)
                    t0 += STAGES[name][0]

            class Between:

                def __init__(self, table, engine):
                    self.gens = [pieces(stages, table, engine) for _, _, stages in groups]
                    self.next = [next(gen, None) for gen in self.gens]

                def __call__(self, u):
                    for k, (first, last, stages) in enumerate(groups):
                        total = sum(STAGES[name][0] for name, _ in stages)
                        tick = min(total, (u - first + 1) * total // (last - first)) if u >= first else 0
                        while self.next[k] is not None and self.next[k] < tick:
                            self.next[k] = next(self.gens[k], None)

                def finish(self):
                    for gen in self.gens:
                        for _ in gen:
                            pass

            with nc.Block() as block:
                @block.sync
                def _(sp):
                    def l0_pre_sync_(b, t0):
                        if "l0_post" in names:
                            sp.wait_ge(S["res_0"], 1)
                        l0_pre_sync(sp, b)
                        yield t0 + 8
                        prep_sync(sp, scans, 0, count["l0_pre"])
                        sp.wait_ge(S["x_in"], 16)
                        sp.wait_ge(S["row_in"], 16)

                    def l1_post_sync_(b, t0):
                        l1_post_sync(sp, b)
                        yield t0 + 5
                        sp.wait_ge(S["gate_in"], 16)

                    def prep1_sync_(b, t0):
                        prep_sync(sp, scans, 1, count["prep1"])
                        yield t0 + 1

                    def l1_pre_sync_(b, t0):
                        yield t0 + 9
                        prep_sync(sp, scans, 2, count["l1_pre"])

                    def l2_sync_(b, t0):
                        l2_sync(sp, b)
                        yield t0 + 4
                        sp.wait_ge(S["key_in"], 16)

                    def l3_sync_(b, t0):
                        sp.wait_ge(S["k_sb"], 4)
                        l3_sync(sp, b)
                        yield t0 + 16
                        sp.wait_ge(S["mask_in"], 16)
                        sp.wait_ge(S["res_3"], 1)
                        sp.dma_start(out[bass.ds(b, 1)].rearrange("b (k p) d -> p (b k) d", p=P),
                                     x2[:, :, :]).then_inc(S["out_done"], 16)
                        sp.wait_ge(S["out_done"], 16)

                    between = Between({"l0_pre": l0_pre_sync_, "prep1": prep1_sync_, "l1_post": l1_post_sync_,
                                       "l1_pre": l1_pre_sync_, "l2": l2_sync_, "l3": l3_sync_}, SYNC)
                    if scans:
                        scans.sync(sp, between)
                    between.finish()
                    if scans:
                        scans.wait_c(sp)

                @block.tensor
                def _(pe):
                    between = Between({"l0_post": lambda b, t0: l0_post_tensor(pe, t0),
                                       "l0_pre": lambda b, t0: l0_pre_tensor(pe, count["l0_pre"], t0),
                                       "prep1": lambda b, t0: prep_tensor(pe, 1, count["prep1"], t0),
                                       "l1_post": lambda b, t0: l1_post_tensor(pe, t0),
                                       "l1_pre": lambda b, t0: l1_pre_tensor(pe, count["l1_pre"], t0),
                                       "l2": lambda b, t0: l2_tensor(pe, t0), "l3": lambda b, t0: l3_tensor(pe, t0)}, TENSOR)
                    if scans:
                        scans.tensor(pe, between)
                    between.finish()

                @block.scalar
                def _(act):
                    act_chain[0] = Chain(act, S["act_chain"])
                    between = Between({"l0_pre": lambda b, t0: l0_pre_scalar(act, count["l0_pre"], t0),
                                       "prep1": lambda b, t0: prep_scalar(act, 1, count["prep1"], t0),
                                       "l1_post": lambda b, t0: l1_post_scalar(act, t0),
                                       "l1_pre": lambda b, t0: l1_pre_scalar(act, count["l1_pre"], t0),
                                       "l2": lambda b, t0: l2_scalar(act, t0), "l3": lambda b, t0: l3_scalar(act, t0)}, SCALAR)
                    if scans:
                        scans.scalar(act, between)
                    between.finish()

                @block.vector
                def _(dve):
                    ch = Chain(dve, S["dve_chain"])
                    between = Between({"l0_post": lambda b, t0: l0_post_vector(dve, ch, t0),
                                       "l0_pre": lambda b, t0: l0_pre_vector(dve, ch, count["l0_pre"], t0),
                                       "prep1": lambda b, t0: prep_vector(dve, ch, 1, count["prep1"], T - 1, t0),
                                       "l1_post": lambda b, t0: l1_post_vector(dve, ch, t0),
                                       "l1_pre": lambda b, t0: l1_pre_vector(dve, ch, b, count["l1_pre"], t0),
                                       "l2": lambda b, t0: l2_vector(dve, ch, b, t0), "l3": lambda b, t0: l3_vector(dve, ch, t0)},
                                      VECTOR)
                    if scans:
                        scans.vector(dve, between)
                    between.finish()

                if scans:
                    @block.gpsimd
                    def _(pool):
                        scans.gpsimd(pool)
            nc.multi_engine_barrier(list(mybir.ALL_ENGINES), sems_to_clear=all_sems)

        FIRST, SECOND, THIRD = (0, 0), (1, 1), (2, 2)
        END = 2 * UNITS + LAG
        LAST = 3 * UNITS

        def early(*stages):
            return (0, 26, [*stages, ("prep1", None)])

        def iteration(i, late):
            run([FIRST, SECOND, THIRD], early(("l1_post", i - 2)), (26, 61, [("l1_pre", i - 1)]),
                (15, LAST + 2, [("l2", i - 2), ("l3", i - 2)]), (END, LAST, late))

        run([], (0, 1, [("l0_pre", 0)]))
        run([FIRST, SECOND], early(), (END, LAST, [("l0_post", 0), ("l0_pre", 1)]))
        run([FIRST, SECOND, THIRD], early(), (26, 61, [("l1_pre", 0)]), (END, LAST, [("l0_post", 1), ("l0_pre", 2)]))
        with nc.Fori(2, B - 1) as i:
            iteration(i, [("l0_post", i), ("l0_pre", i + 1)])
        iteration(B - 1, [("l0_post", B - 1)])
        run([], (0, 1, [("l1_post", B - 2), ("l1_pre", B - 1)]))
        run([(2, 0)], (0, UNITS, [("l2", B - 2), ("l3", B - 2)]))
        run([], (0, 1, [("l1_post", B - 1), ("l2", B - 1), ("l3", B - 1)]))


def pack(inputs):
    f = {k: np.asarray(v) for k, v in inputs.items()}

    def blocks(m):
        k, n = m.shape
        return m.reshape(k // P, P, n).transpose(1, 0, 2).reshape(P, -1)

    def spread(m):
        k = m.shape[0]
        out = np.zeros((k, H2, 32), m.dtype)
        out[:, :, :DH2] = m.reshape(k, H2, DH2)
        return out.reshape(k, H2 * 32)

    def column(v):
        return v.reshape(-1, P).T

    def states(m):
        return m.reshape(EB, P, -1).transpose(1, 0, 2).reshape(P, -1)

    key_row = np.zeros(H2 * 32, np.float32)
    key_row[DH2::32] = 1
    L0, L1, L2, L3 = ("L0_cond_", "L1_cond_", "L2_cond_", "L3_cond_")
    ws = dict(wx=f[L0 + "Wx"].T, wf=f[L0 + "Wf"].T,
              wdlt0=f[L0 + "Wdbc1"][:R].T, wbc0=f[L0 + "Wdbc1"][R:].T,
              wdlt1=f[L0 + "Wdbc2"][:R].T, wbc1=f[L0 + "Wdbc2"][R:].T,
              win=f[L1 + "W_in"], wdlt2=f[L1 + "W_xp"][:, :R], wbc2=f[L1 + "W_xp"][:, R:], wout1=f[L1 + "W_out"],
              wq2=spread(f[L2 + "q_w"]), wk2=spread(f[L2 + "k_w"]), wv2=f[L2 + "v_w"], wo2=f[L2 + "out_w"],
              wq3=f[L3 + "Wq"], wk3=f[L3 + "Wk"], wv3=f[L3 + "Wv"], wo3=f[L3 + "W_out"])
    cs = dict(n2g=column(f[L0 + "norm2_g"]), n2b=column(f[L0 + "norm2_b"]), bx=column(f[L0 + "bx"]),
              bz=column(f[L0 + "bz"]), bc0=column(f[L0 + "bc1"]), bc1=column(f[L0 + "bc2"]),
              bdt0=column(f[L0 + "bdt1"]), bdt1=column(f[L0 + "bdt2"]), bdt2=column(f[L1 + "b_dt"]),
              dp0=column(f[L0 + "Dp1"]), dp1=column(f[L0 + "Dp2"]), dp2=column(f[L1 + "D_param"]),
              alog0=states(f[L0 + "Alog1"]), alog1=states(f[L0 + "Alog2"]), alog2=states(f[L1 + "A_log"]),
              convw=states(f[L1 + "conv_w"].reshape(E, CT)), convb=column(f[L1 + "conv_b"]),
              l2w=column(f[L2 + "norm_w"]), l2b=column(f[L2 + "norm_b"]),
              bq2=column(spread(f[L2 + "q_b"][None])[0] + key_row), bk2=column(spread(f[L2 + "k_b"][None])[0]),
              l3w=column(f[L3 + "ln_w"]), l3b=column(f[L3 + "ln_b"]), bk3=column(f[L3 + "bk"]),
              mask2=column(f["mask_BxS_ff1"].reshape(-1)), mask3=column(f["mask_BxSx1_fk1"].reshape(-1)),
              keyrow=(NEG * key_row[:P])[:, None])
    return {
        "x": f["x"],
        "weights": np.concatenate([blocks(ws[k]) for k in WEIGHTS], 1),
        "columns": np.concatenate([cs[k] for k in COLUMNS], 1),
        "wdt_bias": np.concatenate(
            [np.stack([f[L0 + "Wdt1"].T, f[L0 + "Wdt2"].T, f[L1 + "W_dt"]], 1).reshape(R, 3 * E),
             np.stack([f[L0 + "bf"], f[L2 + "v_b"], f[L2 + "out_b"], f[L3 + "bq"], f[L3 + "bv"],
                       f[L3 + "b_out"]]).reshape(1, 3 * E)]),
        "ada_w": blocks(np.concatenate([f[L0 + "Wada"].T, f[L1 + "W_ada"], f[L2 + "emb_w"], f[L3 + "W_emb"]], 1))
        .reshape(P, CB_, NADA),
        "ada_b": np.concatenate([f[L0 + "bada"], f[L1 + "b_ada"], f[L2 + "emb_b"], f[L3 + "b_emb"]])[None],
        "cond": f["cond_2048"].T.reshape(CB_, P, B).transpose(1, 0, 2),
        "norm_rows": np.stack([f[L0 + "norm1_g"], f[L0 + "norm1_b"], f[L1 + "gamma"], f[L1 + "beta"],
                               f[L2 + "sb_norm_w"], f[L2 + "sb_norm_b"], f[L3 + "ln2_w"], f[L3 + "ln2_b"]]),
        "wz": blocks(f[L0 + "Wz"]).reshape(P, EB, D),
        "wc": np.stack([blocks(f[L0 + "Wc1"].T).reshape(P, EB, E), blocks(f[L0 + "Wc2"].T).reshape(P, EB, E)], 1),
        "itok": f["itok_S_0_1023"],
        "mask2": f["mask_BxS_ff1"],
        "mask3": f["mask_BxSx1_fk1"].reshape(B, T),
    }


def kernel(**inputs):
    import concourse.bacc as _bacc
    from concourse.bass_utils import run_bass_kernel_spmd as _run

    nc = _bacc.Bacc("TRN2", target_bir_lowering=False, num_devices=1)
    arrays, dram = {}, {}
    for name, a in pack(inputs).items():
        a = np.ascontiguousarray(a)
        arrays[f"in_{name}_dram"] = a
        dram[name] = nc.dram_tensor(f"in_{name}_dram", a.shape, mybir.dt.from_np(a.dtype), kind="ExternalInput").ap()
    out = nc.dram_tensor("out_0_dram", (B, T, D), F32, kind="ExternalOutput").ap()
    build(nc, dram, out)
    r = _run(nc, [arrays], core_ids=[0])
    return r.results[0]["out_0_dram"]
```
